# Optimizing a Trainium2 kernel written in Bass

```python
import numpy as np
import jax
import jax.numpy as jnp

def _softmax(x, axis=-1):
    return jax.nn.softmax(x, axis=axis)

def _gelu(x):
    return jax.nn.gelu(x, approximate=True)

def _silu(x):
    return jax.nn.silu(x)

def _sigmoid(x):
    return jax.nn.sigmoid(x)

def _layernorm(x, axis=-1, eps=1e-05):
    m = jnp.mean(x, axis=axis, keepdims=True)
    v = jnp.var(x, axis=axis, keepdims=True)
    return (x - m) / jnp.sqrt(v + eps)

def _scatter_add(tgt, idx, src, axis=0):
    return tgt.at[idx].add(src)

def _segment_sum(src, seg, n):
    return jax.ops.segment_sum(src, seg, n)
kernel_name = 'mk_adaln_attn_ffn_d1_seqx_r8_3b5f33'

def setup_inputs(seed: int=0):
    np.random.seed(seed)
    _w = jnp.asarray

    def _rec_inputs():
        import jax
        import jax.numpy as jnp
        _rk = jax.random.key(seed)
        x = -7.109e-05 + 0.9999 * jax.random.normal(jax.random.fold_in(_rk, 1), (32, 128, 128), jnp.float32)
        _lenS = 128 - jax.random.randint(jax.random.fold_in(_rk, 7), (32,), 0, max(1, 128 // 4) + 1, jnp.int32)
        _lenS2 = 128 - jax.random.randint(jax.random.fold_in(_rk, 8), (32,), 0, max(1, 128 // 4) + 1, jnp.int32)
        cond_512 = 0.0061147 + 1.02565 * jax.random.normal(jax.random.fold_in(_rk, 11), (32, 64), jnp.float32)
        return (x, cond_512)
    x, cond_512 = _rec_inputs()

    def _L0_cond_setup():
        import jax, jax.numpy as jnp
        import numpy as np
        W_DIM = 64
        CLAMP = 256.0
        key = jax.random.key(seed)
        ks = jax.random.split(key, 6)
        B, L, C = (8, 1024, 128)
        return {'x': jax.random.normal(ks[0], (B, L, C), dtype=jnp.float32), 'w': jax.random.normal(ks[1], (B, W_DIM), dtype=jnp.float32), 'weight': jax.random.normal(ks[2], (C, C), dtype=jnp.float32), 'bias': jax.random.normal(ks[3], (C,), dtype=jnp.float32), 'affine_w': jax.random.normal(ks[4], (C, W_DIM), dtype=jnp.float32), 'affine_b': jnp.ones((C,), dtype=jnp.float32)}
    _L0_cond_all = _L0_cond_setup()
    _L0_cond_in = {k: v for k, v in _L0_cond_all.items() if k in ('weight', 'bias', 'affine_w', 'affine_b')}
    del _L0_cond_all

    def _L0_attn_setup():
        import jax, jax.numpy as jnp
        import numpy as np
        import math
        INPUT_WIDTH = 128
        KEY_WIDTH = 64
        VALUE_WIDTH = 64
        NUM_HEADS = 16
        NUM_GROUPS = 4
        HEADS_PER_GROUP = NUM_HEADS // NUM_GROUPS
        key = jax.random.key(seed)
        k_x, k_q, k_k, k_v, k_p = jax.random.split(key, 5)
        n, s = (2, 256)

        def lin(k, fan_in, fan_out):
            bound = 1.0 / math.sqrt(fan_in)
            return jax.random.uniform(k, (fan_in, fan_out), minval=-bound, maxval=bound, dtype=jnp.float32)
        return {'X': jax.random.normal(k_x, (n, s, INPUT_WIDTH), dtype=jnp.float32), 'Wq': lin(k_q, INPUT_WIDTH, NUM_HEADS * KEY_WIDTH), 'Wk': lin(k_k, INPUT_WIDTH, NUM_GROUPS * KEY_WIDTH), 'Wv': lin(k_v, INPUT_WIDTH, NUM_GROUPS * VALUE_WIDTH), 'Wpost': lin(k_p, NUM_HEADS * VALUE_WIDTH, INPUT_WIDTH)}
    _L0_attn_all = _L0_attn_setup()
    _L0_attn_in = {k: v for k, v in _L0_attn_all.items() if k in ('Wq', 'Wk', 'Wv', 'Wpost')}
    del _L0_attn_all

    def _L0_cond2_setup():
        import jax, jax.numpy as jnp
        import numpy as np
        import math
        HEAD_NUM = 16
        EPS = 1e-08

        def modulated_linear(x, s, aff_w, aff_b, w, b):
            style = s @ aff_w.T + aff_b
            w_mod = w[None, :, :] * style[:, None, :]
            demod = jax.lax.rsqrt(jnp.sum(w_mod * w_mod, axis=2) + EPS)
            w_mod = w_mod * demod[:, :, None]
            return jnp.einsum('bni,boi->bno', x, w_mod) + b
        key = jax.random.key(seed)
        ks = jax.random.split(key, 6)
        B, N, F, S = (8, 128, 128, 64)
        return {'x': jax.random.normal(ks[0], (B, N, F), dtype=jnp.float32), 's': jax.random.normal(ks[1], (B, S), dtype=jnp.float32), 'k_aff_w': jax.random.normal(ks[2], (F, S), dtype=jnp.float32) * 0.02, 'k_aff_b': jnp.ones((F,), dtype=jnp.float32), 'k_w': jax.random.normal(ks[3], (F, F), dtype=jnp.float32) * 0.02, 'k_b': jnp.zeros((F,), dtype=jnp.float32), 'o_aff_w': jax.random.normal(ks[4], (F, S), dtype=jnp.float32) * 0.02, 'o_aff_b': jnp.ones((F,), dtype=jnp.float32), 'o_w': jax.random.normal(ks[5], (F, F), dtype=jnp.float32) * 0.02, 'o_b': jnp.zeros((F,), dtype=jnp.float32)}
    _L0_cond2_all = _L0_cond2_setup()
    _L0_cond2_in = {k: v for k, v in _L0_cond2_all.items() if k in ('k_aff_w', 'k_aff_b', 'k_w', 'k_b', 'o_aff_w', 'o_aff_b', 'o_w', 'o_b')}
    del _L0_cond2_all

    def _L0_ffn_setup():
        import jax, jax.numpy as jnp
        import numpy as np
        HIDDEN = 128
        NUM_EXPERTS = 8
        CAPACITY_FACTOR = 1.25
        key = jax.random.key(seed)
        k_tok, k_g, k_w1, k_b1, k_w2, k_b2 = jax.random.split(key, 6)
        B, S, H, E = (4, 256, HIDDEN, NUM_EXPERTS)
        tokens = jax.random.normal(k_tok, (B, S, H), dtype=jnp.float32)
        gate_w = jax.random.normal(k_g, (E, H), dtype=jnp.float32) * 0.02
        W1 = jax.random.normal(k_w1, (E, H, H), dtype=jnp.float32) * 0.02
        b1 = jax.random.normal(k_b1, (E, H), dtype=jnp.float32) * 0.02
        W2 = jax.random.normal(k_w2, (E, H, H), dtype=jnp.float32) * 0.02
        b2 = jax.random.normal(k_b2, (E, H), dtype=jnp.float32) * 0.02
        return {'tokens': tokens, 'gate_w': gate_w, 'W1': W1, 'b1': b1, 'W2': W2, 'b2': b2}
    _L0_ffn_all = _L0_ffn_setup()
    _L0_ffn_in = {k: v for k, v in _L0_ffn_all.items() if k in ('gate_w', 'W1', 'b1', 'W2', 'b2')}
    del _L0_ffn_all
    return {'x': x, 'cond_512': cond_512, 'L0_cond_weight': _L0_cond_in['weight'], 'L0_cond_bias': _L0_cond_in['bias'], 'L0_cond_affine_w': _L0_cond_in['affine_w'], 'L0_cond_affine_b': _L0_cond_in['affine_b'], 'L0_attn_Wq': _L0_attn_in['Wq'], 'L0_attn_Wk': _L0_attn_in['Wk'], 'L0_attn_Wv': _L0_attn_in['Wv'], 'L0_attn_Wpost': _L0_attn_in['Wpost'], 'L0_cond2_k_aff_w': _L0_cond2_in['k_aff_w'], 'L0_cond2_k_aff_b': _L0_cond2_in['k_aff_b'], 'L0_cond2_k_w': _L0_cond2_in['k_w'], 'L0_cond2_k_b': _L0_cond2_in['k_b'], 'L0_cond2_o_aff_w': _L0_cond2_in['o_aff_w'], 'L0_cond2_o_aff_b': _L0_cond2_in['o_aff_b'], 'L0_cond2_o_w': _L0_cond2_in['o_w'], 'L0_cond2_o_b': _L0_cond2_in['o_b'], 'L0_ffn_gate_w': _L0_ffn_in['gate_w'], 'L0_ffn_W1': _L0_ffn_in['W1'], 'L0_ffn_b1': _L0_ffn_in['b1'], 'L0_ffn_W2': _L0_ffn_in['W2'], 'L0_ffn_b2': _L0_ffn_in['b2']}

def reference(x, cond_512, L0_cond_weight, L0_cond_bias, L0_cond_affine_w, L0_cond_affine_b, L0_attn_Wq, L0_attn_Wk, L0_attn_Wv, L0_attn_Wpost, L0_cond2_k_aff_w, L0_cond2_k_aff_b, L0_cond2_k_w, L0_cond2_k_b, L0_cond2_o_aff_w, L0_cond2_o_aff_b, L0_cond2_o_w, L0_cond2_o_b, L0_ffn_gate_w, L0_ffn_W1, L0_ffn_b1, L0_ffn_W2, L0_ffn_b2):
    import jax
    import jax.numpy as jnp

    def _L0_cond_ref(x, w, weight, bias, affine_w, affine_b):
        import jax, jax.numpy as jnp
        import numpy as np
        W_DIM = 64
        CLAMP = 256.0
        B, L, C = x.shape
        gain = 1.0 / np.sqrt(W_DIM).astype(np.float32)
        styles = w @ (affine_w * gain).T + affine_b
        ws = weight[None, :, :] * styles[:, None, :]
        dcoefs = jax.lax.rsqrt(jnp.sum(ws * ws, axis=2) + 1e-08)
        xm = x * styles[:, None, :]
        y = jnp.einsum('blc,oc->blo', xm, weight)
        y = y * dcoefs[:, None, :]
        y = jnp.clip(y + bias, -CLAMP, CLAMP)
        return y

    def _L0_attn_ref(X, Wq, Wk, Wv, Wpost):
        import jax, jax.numpy as jnp
        import numpy as np
        import math
        INPUT_WIDTH = 128
        KEY_WIDTH = 64
        VALUE_WIDTH = 64
        NUM_HEADS = 16
        NUM_GROUPS = 4
        HEADS_PER_GROUP = NUM_HEADS // NUM_GROUPS
        n, s, _ = X.shape
        Q = (X @ Wq).reshape(n, s, NUM_GROUPS, HEADS_PER_GROUP, KEY_WIDTH)
        K = (X @ Wk).reshape(n, s, NUM_GROUPS, KEY_WIDTH)
        V = (X @ Wv).reshape(n, s, NUM_GROUPS, VALUE_WIDTH)
        scale = 1.0 / math.sqrt(KEY_WIDTH)
        raw = jnp.einsum('bsgwe,btge->bstgw', Q, K * scale)
        attn = jax.nn.softmax(raw, axis=2)
        A = jnp.einsum('bstgw,btge->bsgwe', attn, V).reshape(n, s, NUM_HEADS * VALUE_WIDTH)
        P = A @ Wpost
        return X + P

    def _L0_cond2_ref(x, s, k_aff_w, k_aff_b, k_w, k_b, o_aff_w, o_aff_b, o_w, o_b):
        import jax, jax.numpy as jnp
        import numpy as np
        import math
        HEAD_NUM = 16
        EPS = 1e-08

        def modulated_linear(x, s, aff_w, aff_b, w, b):
            style = s @ aff_w.T + aff_b
            w_mod = w[None, :, :] * style[:, None, :]
            demod = jax.lax.rsqrt(jnp.sum(w_mod * w_mod, axis=2) + EPS)
            w_mod = w_mod * demod[:, :, None]
            return jnp.einsum('bni,boi->bno', x, w_mod) + b
        B, N, F = x.shape
        H = HEAD_NUM
        D = F // H
        kx = modulated_linear(x, s, k_aff_w, k_aff_b, k_w, k_b)
        kx = kx.reshape(B, N, H, D)
        q = k = v = kx
        scores = jnp.einsum('bnhd,bnjd->bnhj', q, k) / math.sqrt(D)
        A = jax.nn.softmax(scores, axis=-1)
        out = jnp.einsum('bnhj,bnjd->bnhd', A, v).reshape(B, N, F)
        out = modulated_linear(out, s, o_aff_w, o_aff_b, o_w, o_b)
        return out

    def _L0_ffn_ref(tokens, gate_w, W1, b1, W2, b2):
        import jax, jax.numpy as jnp
        import numpy as np
        HIDDEN = 128
        NUM_EXPERTS = 8
        CAPACITY_FACTOR = 1.25
        B, S, H = tokens.shape
        E = gate_w.shape[0]
        T = B * S
        x = tokens.reshape(T, H)
        logits = x @ gate_w.T
        probs = jax.nn.softmax(logits, axis=-1)
        top2_w, top2_idx = jax.lax.top_k(probs, 2)
        cap = int(CAPACITY_FACTOR * T / E)
        counts = jnp.bincount(top2_idx.reshape(-1), length=E)
        keep = (counts <= cap).astype(x.dtype)
        comb = jnp.zeros((T, E), dtype=x.dtype).at[jnp.arange(T)[:, None], top2_idx].add(top2_w)
        comb = comb * keep[None, :]
        h = jax.nn.relu(jnp.einsum('th,ehf->tef', x, W1) + b1[None, :, :])
        y = jnp.einsum('teh,ehf->tef', h, W2) + b2[None, :, :]
        out = jnp.einsum('te,tef->tf', comb, y)
        return out.reshape(B, S, H)
    x = x + _L0_attn_ref(_L0_cond_ref(x, cond_512, L0_cond_weight, L0_cond_bias, L0_cond_affine_w, L0_cond_affine_b), L0_attn_Wq, L0_attn_Wk, L0_attn_Wv, L0_attn_Wpost)
    x = x + _L0_ffn_ref(_L0_cond2_ref(x, cond_512, L0_cond2_k_aff_w, L0_cond2_k_aff_b, L0_cond2_k_w, L0_cond2_k_b, L0_cond2_o_aff_w, L0_cond2_o_aff_b, L0_cond2_o_w, L0_cond2_o_b), L0_ffn_gate_w, L0_ffn_W1, L0_ffn_b1, L0_ffn_W2, L0_ffn_b2)
    return x

_drawn_inputs = setup_inputs


def setup_inputs(seed=0):
    import zlib

    import numpy as np

    out = dict(_drawn_inputs(seed))
    spreads = {'L0_cond_affine_b': (1.0, 0.2),
     'L0_cond2_k_aff_b': (1.0, 0.6),
     'L0_cond2_k_b': (0.0, 0.8),
     'L0_cond2_o_aff_b': (1.0, 0.6),
     'L0_cond2_o_b': (0.0, 0.8)}
    factors = {'L0_attn_Wq': 3.39,
     'L0_attn_Wk': 3.373,
     'L0_cond2_k_aff_w': 8.0,
     'L0_cond2_k_w': 8.0,
     'L0_cond2_o_aff_w': 8.0,
     'L0_cond2_o_w': 8.0,
     'L0_ffn_gate_w': 8.0,
     'L0_ffn_W1': 8.0,
     'L0_ffn_b1': 21.369,
     'L0_ffn_W2': 8.0,
     'L0_ffn_b2': 25.089}
    for name, (base, spread) in spreads.items():
        noise = np.random.default_rng([zlib.crc32(name.encode()), seed]).standard_normal(out[name].shape)
        drawn = base * np.exp(spread * noise) if base else spread * noise
        out[name] = jnp.asarray(drawn.astype(out[name].dtype))
    for name, factor in factors.items():
        out[name] = (out[name] * factor).astype(out[name].dtype)
    return out
```

```python
from contextlib import ExitStack

import numpy as np

import concourse.bass as bass
from concourse import mybir

F32 = mybir.dt.float32
BF16 = mybir.dt.bfloat16
I32 = mybir.dt.int32
ALU = mybir.AluOpType
ACT = mybir.ActivationFunctionType
AX = mybir.AxisListType

P = 128
BATCH = 32
TOKENS = BATCH * P
COND = 64
GROUPS, HPG, KEY = 4, 4, 64
HEADS = GROUPS * HPG
CHUNKS = HEADS * KEY // P
MH, MD = 16, 8
SHIFTS = MH // 2 + 1
EXPERTS = 8
CAP = int(1.25 * TOKENS / EXPERTS)
QUAD = 4
QUADS = BATCH // QUAD
CLAMP = 256.0
EPS = 1e-8
KEY_SCALE = 1.0 / KEY ** 0.5
MIX_SCALE = 1.0 / MD ** 0.5
LOOP_FROM, LOOP_TO = 4, BATCH - 2


def build(nc, xT, condT, aff_wT, aff_b, mod_wT, mod_b, wq, wk, wv, wpost, gate_wT,
          w1, b1T, w2, b2, out):
    ctx = ExitStack()
    with ctx:
        def sb(name, shape, dt=F32):
            return ctx.enter_context(nc.sbuf_tensor(name, shape, dt))

        def pb(name, shape, dt=F32):
            return ctx.enter_context(nc.psum_tensor(name, shape, dt))

        def sem(name):
            return ctx.enter_context(nc.semaphore(name))

        x_all = sb("x_all", [P, TOKENS])
        tok_all = sb("tok_all", [P, TOKENS])
        acc_all = sb("acc_all", [P, BATCH, P])
        logits = sb("logits", [P, BATCH, EXPERTS])
        ident = sb("ident", [P, P])
        ones = sb("ones", [P, P])
        pick = sb("pick", [P, HEADS, P], BF16)
        cond_sb = sb("cond_sb", [COND, BATCH])
        affw_sb = sb("affw_sb", [COND, 3, P])
        affb_sb = sb("affb_sb", [P, 3])
        modw_sb = sb("modw_sb", [P, 3, P])
        modb_sb = sb("modb_sb", [P, 3])
        wq_sb = sb("wq_sb", [P, HEADS * KEY])
        wk_sb = sb("wk_sb", [P, GROUPS * KEY])
        wv_sb = sb("wv_sb", [P, GROUPS * KEY])
        wpost_sb = sb("wpost_sb", [P, CHUNKS, P])
        gate_sb = sb("gate_sb", [P, EXPERTS])
        w1_sb = sb("w1_sb", [P, EXPERTS, P])
        w2_sb = sb("w2_sb", [P, EXPERTS, P])
        b1_sb = sb("b1_sb", [P, EXPERTS])
        b2_rows = sb("b2_rows", [P, P // EXPERTS, P])
        style = sb("style", [P, 3, BATCH])
        demod = sb("demod", [P, 3, BATCH])
        style_sq = sb("style_sq", [P, 3, BATCH])
        modw_sq = sb("modw_sq", [P, 3, P])
        power = sb("power", [P, 3, BATCH])
        root = sb("root", [P, 3, BATCH])
        inv_root = sb("inv_root", [P, 3, BATCH])
        newton = sb("newton", [P, 3, BATCH])
        xs = sb("xs", [P, 2, P])
        y_raw = sb("y_raw", [P, P])
        yT = sb("yT", [P, P])
        qT = sb("qT", [P, 2, CHUNKS, P])
        q16 = sb("q16", [P, 2, CHUNKS, P], BF16)
        k_pad = sb("k_pad", [P, 2, GROUPS, 2, P])
        k16 = sb("k16", [P, 2, GROUPS, 2, P], BF16)
        v1 = sb("v1", [P, 2, GROUPS, KEY + 1])
        row_max = sb("row_max", [P, P])
        neg_max = sb("neg_max", [P, P], BF16)
        prob = sb("prob", [P, 2, HPG, P])
        recip_den = sb("recip_den", [P, 2, HPG])
        att = sb("att", [P, HEADS, KEY])
        attT = sb("attT", [P, CHUNKS, P])
        x1T = sb("x1T", [P, P])
        x1s = sb("x1s", [P, P])
        kxT = sb("kxT", [P, P])
        kx2 = sb("kx2", [P, 2, 2 * P])
        pair = sb("pair", [P, SHIFTS, P])
        score = sb("score", [P, MH, 2 * MH])
        h_max = sb("h_max", [P, MH])
        shifted = sb("shifted", [P, MH, MH])
        weight = sb("weight", [P, 2, MH, MH])
        h_den = sb("h_den", [P, MH])
        h_rden = sb("h_rden", [P, MH])
        mix_lo = sb("mix_lo", [P, MH // 2, P])
        mix_hi = sb("mix_hi", [P, MH // 2, P])
        mix_sum = sb("mix_sum", [P, P])
        mix = sb("mix", [P, P])
        mixT = sb("mixT", [P, P])
        tokT = sb("tokT", [P, P])
        r_max = sb("r_max", [P, BATCH])
        r_key = sb("r_key", [P, BATCH])
        gates = sb("gates", [P, BATCH, EXPERTS])
        rest = sb("rest", [P, BATCH, EXPERTS])
        cand = sb("cand", [P, BATCH, EXPERTS])
        first = sb("first", [P, BATCH, EXPERTS])
        chosen = sb("chosen", [P, BATCH, EXPERTS])
        rank8 = sb("rank8", [P, EXPERTS])
        index8 = sb("index8", [P, EXPERTS])
        before = sb("before", [P, EXPERTS, EXPERTS])
        count = sb("count", [P, EXPERTS])
        keep = sb("keep", [P, EXPERTS])
        t88 = sb("t88", [P, EXPERTS, EXPERTS])
        place = sb("place", [P, EXPERTS])
        drop_place = sb("drop_place", [P, EXPERTS])
        kept = sb("kept", [P, 1])
        order_f = sb("order_f", [P, EXPERTS])
        order = sb("order", [P, EXPERTS], I32)
        n_run = sb("n_run", [P, 2], I32)
        gatesT = sb("gatesT", [P, 2, P])
        w1_now = sb("w1_now", [P, P])
        b1_now = sb("b1_now", [P, 1])
        hT = sb("hT", [P, 2, QUAD * P])

        bank_s = [pb(f"bank_s{i}", [P, HPG, P]) for i in range(2)]
        bank_t = [pb(f"bank_t{i}", [P, HPG, P]) for i in range(2)]
        bank_a = [pb(f"bank_a{i}", [P, 512]) for i in range(2)]
        misc = [pb(f"misc{i}", [P, QUAD, P]) for i in range(2)]

        def att_bank(g):
            return bank_a[g % 2][:, 0:HPG * (KEY + 1)].rearrange("p (w e) -> p w e", e=KEY + 1)

        s_ld_mod, s_ld_modw, s_ld_x0, s_ld_x, s_ld_qkv = (sem("ld_mod"), sem("ld_modw"), sem("ld_x0"),
                                                         sem("ld_x"), sem("ld_qkv"))
        s_ld_post, s_ld_ffn = sem("ld_post"), sem("ld_ffn")
        s_out = sem("out_written")
        s_const, s_blank, s_zero = sem("const"), sem("blank"), sem("zero")
        s_style_mm, s_style, s_sq, s_power_mm = sem("style_mm"), sem("style"), sem("sq"), sem("power_mm")
        s_power, s_root, s_demod = sem("power"), sem("root"), sem("demod")
        s_xs, s_y_mm, s_y_raw, s_yT, s_xy = sem("xs"), sem("y_mm"), sem("y_raw"), sem("yT"), sem("xy")
        s_q_mm, s_q, s_kv_mm, s_k, s_v = sem("q_mm"), sem("q"), sem("kv_mm"), sem("k"), sem("v")
        s_q16, s_k16 = sem("q16"), sem("k16")
        s_s_mm, s_max, s_t_mm, s_prob = sem("s_mm"), sem("max"), sem("t_mm"), sem("prob")
        s_av_mm, s_rden, s_att = sem("av_mm"), sem("rden"), sem("att")
        s_neg_mm, s_neg = sem("neg_mm"), sem("neg")
        s_attT_mm, s_attT = sem("attT_mm"), sem("attT")
        s_post_mm, s_x1T, s_x1s, s_kx_mm, s_kxT = sem("post_mm"), sem("x1T"), sem("x1s"), sem("kx_mm"), sem("kxT")
        s_kxn_mm, s_kx2, s_x1n_mm, s_x1n = sem("kxn_mm"), sem("kx2"), sem("x1n_mm"), sem("x1n")
        s_pair, s_score, s_twice, s_mirror = sem("pair"), sem("score"), sem("twice"), sem("mirror")
        s_hmax, s_shifted, s_weight = sem("hmax"), sem("shifted"), sem("weight")
        s_hden, s_hrden, s_lo, s_hi = sem("hden"), sem("hrden"), sem("lo"), sem("hi")
        s_msum, s_mix, s_mixT_mm, s_mixT = sem("msum"), sem("mix"), sem("mixT_mm"), sem("mixT")
        s_o_mm, s_tok, s_tok_kept, s_log_mm, s_log = (sem("o_mm"), sem("tok"), sem("tok_kept"),
                                                      sem("log_mm"), sem("log"))
        s_rt, s_rt_exp, s_cnt_mm, s_gT_mm, s_gT = sem("rt"), sem("rt_exp"), sem("cnt_mm"), sem("gT_mm"), sem("gT")
        s_b2_mm = sem("b2_mm")
        s_w1, s_h_mm, s_h, s_e_mm = sem("w1"), sem("h_mm"), sem("h"), sem("e_mm")
        s_e = sem("e")

        ROUTE_STEPS = {}

        def n(b):
            return b + 1

        def need(eng, s, v):
            if not (isinstance(v, int) and v <= 0):
                eng.wait_ge(s, v)

        def has(b):
            return not isinstance(b, int) or 0 <= b < BATCH

        def bank_users(bank, s):
            a, c, d = s + 1, s - 1, s - 2
            return ((("y", a, [(s_y_raw, n(a))]), ("q0", a, [(s_q, 2 * a + 1)]), ("kx", c, [(s_kxT, n(c))]),
                     ("kxn", c, [(s_kx2, n(c))]), ("x1n", c, [(s_x1n, n(c))]), ("o", d, [(s_tok, n(d))]),
                     ("att0", s, [(s_attT, 2 * s + 1)])),
                    (("post", c, [(s_x1T, n(c))]), ("neg", s, [(s_neg, n(s))]), ("q1", a, [(s_q, 2 * a + 2)]),
                     ("kv", a, [(s_v, n(a)), (s_k, 4 * n(a))]), ("mix", d, [(s_mixT, n(d))]),
                     ("log", d, [(s_log, n(d))]), ("att1", s, [(s_attT, 2 * s + 2)])))[bank]

        def bank_free(eng, bank, s, use):
            now = bank_users(bank, s)
            at = [u[0] for u in now].index(use)
            for _, b, readers in (*reversed(now[:at]), *reversed(bank_users(bank, s - 1))):
                if has(b):
                    for sm, v in readers:
                        eng.wait_ge(sm, v)
                    return

        def slots(eng, slot):
            for s in range(-1, LOOP_FROM):
                slot(s, s % 2)
            with eng.Fori(LOOP_FROM // 2, LOOP_TO // 2) as two:
                slot(two * 2, 0)
                slot(two * 2 + 1, 1)
            for s in range(LOOP_TO, BATCH + 2):
                slot(s, s % 2)

        def col(b):
            return bass.ds(b * P, P)

        block = ctx.enter_context(nc.Block())

        @block.vector
        def _(dve):
            V = nc.vector
            V.memset(ones[:, :], 1.0).then_inc(s_zero, 1)
            V.memset(b2_rows[:, :, :], 0.0).then_inc(s_zero, 1)
            V.memset(k_pad[:, :, :, :, :], 0.0).then_inc(s_zero, 1)
            V.memset(v1[:, :, :, :], 1.0).then_inc(s_zero, 1)
            V.memset(row_max[:, :], 0.0).then_inc(s_zero, 1)

            dve.wait_ge(s_ld_modw, 16)
            V.tensor_tensor(modw_sq[:, :, :], modw_sb[:, :, :], modw_sb[:, :, :], ALU.mult).then_inc(s_sq, 1)
            dve.wait_ge(s_style, 3)
            V.tensor_tensor(style_sq[:, :, :], style[:, :, :], style[:, :, :], ALU.mult).then_inc(s_sq, 1)
            dve.wait_ge(s_power_mm, 1)
            V.tensor_scalar(power[:, :, :], misc[1][:, 0, 0:3 * BATCH].rearrange("p (m b) -> p m b", m=3),
                            EPS, None, ALU.add).then_inc(s_power, 1)
            dve.wait_ge(s_root, 1)
            V.reciprocal(inv_root[:, :, :], root[:, :, :]).then_inc(s_demod, 1)
            dve.wait_ge(s_demod, 1)
            V.tensor_tensor(newton[:, :, :], inv_root[:, :, :], inv_root[:, :, :], ALU.mult).then_inc(s_demod, 1)
            dve.wait_ge(s_demod, 2)
            V.tensor_tensor(newton[:, :, :], newton[:, :, :], power[:, :, :], ALU.mult).then_inc(s_demod, 1)
            dve.wait_ge(s_demod, 3)
            V.tensor_scalar(newton[:, :, :], newton[:, :, :], -0.5, 1.5, ALU.mult, ALU.add).then_inc(s_demod, 1)
            dve.wait_ge(s_demod, 4)
            V.tensor_tensor(demod[:, :, :], newton[:, :, :], inv_root[:, :, :], ALU.mult).then_inc(s_demod, 1)
            dve.wait_ge(s_zero, 5)

            def group_max(s, g):
                dve.wait_ge(s_s_mm, 4 * s + g + 1)
                need(dve, s_neg_mm, n(s - 1))
                V.tensor_reduce(row_max[:, HPG * g:HPG * (g + 1)], bank_s[g % 2][:, :, :], AX.X,
                                ALU.max).then_inc(s_max, 1)

            def normalise(s, g):
                dve.wait_ge(s_av_mm, 4 * s + g + 1)
                need(dve, s_att, 4 * s + g - 1)
                V.reciprocal(recip_den[:, g % 2, :].unsqueeze(2), att_bank(g)[:, :, KEY:KEY + 1]).then_inc(s_rden, 1)
                need(dve, s_attT_mm, 2 * n(s - 1))
                dve.wait_ge(s_rden, 4 * s + g + 1)
                V.tensor_tensor(att[:, HPG * g:HPG * (g + 1), :], att_bank(g)[:, :, 0:KEY],
                                recip_den[:, g % 2, :].unsqueeze(2).to_broadcast([P, HPG, KEY]),
                                ALU.mult).then_inc(s_att, 1)

            def slot(s, j):
                a, c, d = s + 1, s - 1, s - 2
                A, B, C, D = has(a), has(s), has(c), has(d)
                ja, jc, jd = 1 - j, 1 - j, j
                if B:
                    group_max(s, 0)
                if A:
                    dve.wait_ge(s_y_raw, n(a))
                    need(dve, s_kv_mm, n(a - 1))
                    need(dve, s_xy, n(a - 1))
                    V.tensor_scalar(yT[:, :], y_raw[:, :], CLAMP, -CLAMP, ALU.min, ALU.max).then_inc(s_yT, 1)
                if B:
                    group_max(s, 1)
                if A:
                    dve.wait_ge(s_yT, n(a))
                    V.tensor_tensor(x_all[:, col(a)], x_all[:, col(a)], yT[:, :], ALU.add).then_inc(s_xy, 1)
                if C:
                    dve.wait_ge(s_post_mm, n(c))
                    dve.wait_ge(s_xy, n(c))
                    need(dve, s_x1n_mm, n(c - 1))
                    need(dve, s_x1s, n(c - 1))
                    V.tensor_tensor(x1T[:, :], misc[1][:, 0, :], x_all[:, col(c)], ALU.add).then_inc(s_x1T, 1)
                if B:
                    group_max(s, 2)
                    group_max(s, 3)
                if D:
                    dve.wait_ge(s_weight, n(d))
                    need(dve, s_mix, n(d - 1))
                    V.tensor_tensor(mix_lo[:, :, :].rearrange("p r (h e) -> p r h e", e=MD),
                                    weight[:, jd, 0:MH // 2, :].unsqueeze(3).to_broadcast([P, MH // 2, MH, MD]),
                                    bass.AP(kx2, jd * 2 * P, [[4 * P, P], [MD, MH // 2], [MD, MH], [1, MD]]),
                                    ALU.mult).then_inc(s_lo, 1)
                    V.tensor_reduce(h_den[:, :], weight[:, jd, :, :].rearrange("p r h -> p h r"), AX.X,
                                    ALU.add).then_inc(s_hden, 1)
                    dve.wait_ge(s_lo, 4 * d + 1)
                    V.tensor_tensor(mix_lo[:, 0:4, :], mix_lo[:, 0:4, :], mix_lo[:, 4:8, :], ALU.add).then_inc(s_lo, 1)
                    dve.wait_ge(s_hden, n(d))
                    V.reciprocal(h_rden[:, :], h_den[:, :]).then_inc(s_hrden, 1)
                    dve.wait_ge(s_lo, 4 * d + 2)
                    V.tensor_tensor(mix_lo[:, 0:2, :], mix_lo[:, 0:2, :], mix_lo[:, 2:4, :], ALU.add).then_inc(s_lo, 1)
                    dve.wait_ge(s_lo, 4 * d + 3)
                    V.tensor_tensor(mix_lo[:, 0, :], mix_lo[:, 0, :], mix_lo[:, 1, :], ALU.add).then_inc(s_lo, 1)
                    dve.wait_ge(s_lo, 4 * d + 4)
                    dve.wait_ge(s_hi, 4 * d + 4)
                    V.tensor_tensor(mix_sum[:, :], mix_lo[:, 0, :], mix_hi[:, 0, :], ALU.add).then_inc(s_msum, 1)
                    dve.wait_ge(s_hrden, n(d))
                    dve.wait_ge(s_msum, n(d))
                    need(dve, s_mixT_mm, n(d - 1))
                    V.tensor_tensor(mix[:, :].rearrange("p (h e) -> p h e", e=MD),
                                    mix_sum[:, :].rearrange("p (h e) -> p h e", e=MD),
                                    h_rden[:, :].unsqueeze(2).to_broadcast([P, MH, MD]), ALU.mult).then_inc(s_mix, 1)
                if B:
                    normalise(s, 0)
                    normalise(s, 1)
                if C:
                    dve.wait_ge(s_pair, n(c))
                    need(dve, s_shifted, n(c - 1))
                    V.tensor_reduce(score[:, 0:SHIFTS, 0:MH], pair[:, :, :].rearrange("p r (h e) -> p r h e", e=MD),
                                    AX.X, ALU.add).then_inc(s_score, 1)
                if B:
                    normalise(s, 2)
                if C:
                    dve.wait_ge(s_score, n(c))
                    V.tensor_copy(score[:, 1:MH // 2, MH:2 * MH], score[:, 1:MH // 2, 0:MH]).then_inc(s_twice, 1)
                    dve.wait_ge(s_twice, n(c))
                    top = MH // 2 - 1
                    V.tensor_copy(score[:, SHIFTS:MH, 0:MH],
                                  bass.AP(score, top * (2 * MH - 1) + MH,
                                          [[2 * MH * MH, P], [-(2 * MH - 1), top], [1, MH]])).then_inc(s_mirror, 1)
                if B:
                    normalise(s, 3)
                if C:
                    dve.wait_ge(s_mirror, n(c))
                    V.tensor_reduce(h_max[:, :], score[:, :, 0:MH].rearrange("p r h -> p h r"), AX.X,
                                    ALU.max).then_inc(s_hmax, 1)
                    dve.wait_ge(s_hmax, n(c))
                    need(dve, s_weight, n(c - 1))
                    V.tensor_tensor(shifted[:, :, :], score[:, :, 0:MH],
                                    h_max[:, :].unsqueeze(1).to_broadcast([P, MH, MH]),
                                    ALU.subtract).then_inc(s_shifted, 1)

            slots(dve, slot)

            steps = [0]

            def step(ins):
                steps[0] += 1
                ins.then_inc(s_rt, 1)
                dve.wait_ge(s_rt, steps[0])
                return steps[0]

            def over_e(t):
                return t[:, :].unsqueeze(2).to_broadcast([P, BATCH, EXPERTS])

            def over_t(t):
                return t[:, :].unsqueeze(1).to_broadcast([P, BATCH, EXPERTS])

            dve.wait_ge(s_log, BATCH)
            step(V.tensor_reduce(r_max[:, :], logits[:, :, :], AX.X, ALU.max))
            ROUTE_STEPS["exp"] = step(V.tensor_tensor(rest[:, :, :], logits[:, :, :], over_e(r_max), ALU.subtract))
            dve.wait_ge(s_rt_exp, 1)
            step(V.tensor_reduce(r_key[:, :], gates[:, :, :], AX.X, ALU.add))
            step(V.reciprocal(r_max[:, :], r_key[:, :]))
            step(V.tensor_tensor(gates[:, :, :], gates[:, :, :], over_e(r_max), ALU.mult))

            def choose(src, dst):
                step(V.tensor_reduce(r_max[:, :], src[:, :, :], AX.X, ALU.max))
                step(V.tensor_tensor(cand[:, :, :], src[:, :, :], over_e(r_max), ALU.is_equal))
                step(V.tensor_tensor(cand[:, :, :], cand[:, :, :], over_t(rank8), ALU.mult))
                step(V.tensor_reduce(r_key[:, :], cand[:, :, :], AX.X, ALU.max))
                step(V.tensor_tensor(dst[:, :, :], over_t(rank8), over_e(r_key), ALU.is_equal))

            dve.wait_ge(s_const, 4)
            choose(gates, first)
            step(V.scalar_tensor_tensor(out=rest[:, :, :], in0=first[:, :, :], scalar=-2.0, in1=gates[:, :, :],
                                        op0=ALU.mult, op1=ALU.add))
            choose(rest, chosen)
            step(V.tensor_tensor(chosen[:, :, :], chosen[:, :, :], first[:, :, :], ALU.add))
            ROUTE_STEPS["count"] = step(V.tensor_reduce(count[:, :], chosen[:, :, :].rearrange("p t e -> p e t"),
                                                        AX.X, ALU.add))
            step(V.tensor_tensor(gates[:, :, :], gates[:, :, :], chosen[:, :, :], ALU.mult))
            dve.wait_ge(s_cnt_mm, 1)
            step(V.tensor_scalar(keep[:, :], misc[0][:, 0, 0:EXPERTS], float(CAP), None, ALU.is_le))
            ROUTE_STEPS["gates"] = step(V.tensor_tensor(gates[:, :, :], gates[:, :, :], over_t(keep), ALU.mult))
            wide = [P, EXPERTS, EXPERTS]
            step(V.tensor_tensor(t88[:, :, :], before[:, :, :], keep[:, :].unsqueeze(1).to_broadcast(wide), ALU.mult))
            step(V.tensor_reduce(place[:, :], t88[:, :, :], AX.X, ALU.add))
            step(V.tensor_reduce(kept[:, :], keep[:, :], AX.X, ALU.add))
            step(V.tensor_tensor(drop_place[:, :], index8[:, :], place[:, :], ALU.subtract))
            step(V.tensor_scalar(drop_place[:, :], drop_place[:, :], kept[:, 0:1], None, ALU.add))
            step(V.tensor_tensor(place[:, :], place[:, :], drop_place[:, :], ALU.subtract))
            step(V.tensor_tensor(place[:, :], place[:, :], keep[:, :], ALU.mult))
            step(V.tensor_tensor(place[:, :], place[:, :], drop_place[:, :], ALU.add))
            step(V.tensor_tensor(t88[:, :, :], index8[:, :].unsqueeze(2).to_broadcast(wide),
                                 place[:, :].unsqueeze(1).to_broadcast(wide), ALU.is_equal))
            step(V.tensor_tensor(t88[:, :, :], t88[:, :, :], index8[:, :].unsqueeze(1).to_broadcast(wide), ALU.mult))
            step(V.tensor_reduce(order_f[:, :], t88[:, :, :], AX.X, ALU.add))
            step(V.tensor_copy(order[:, :], order_f[:, :]))
            step(V.tensor_scalar(n_run[:, 0:1], kept[:, :], 2.0, None, ALU.max))
            ROUTE_STEPS["n"] = step(V.tensor_scalar(n_run[:, 1:2], kept[:, :], -1.0, 1.0, ALU.add, ALU.max))

            for q in range(QUADS):
                dve.wait_ge(s_b2_mm, q + 1)
                t = acc_all[:, q * QUAD:(q + 1) * QUAD, :]
                V.tensor_tensor(t, t, bank_s[q % 2][:, :, :], ALU.add).then_inc(s_e, 1)
            dve.wait_ge(s_ld_ffn, 16 * (3 + P // EXPERTS))
            runs = dve.value_load(n_run[0:1, 0:1], min_val=2, max_val=EXPERTS)
            with dve.Fori(0, runs) as k:
                e = dve.value_load(order[0:1, bass.ds(k, 1)], min_val=0, max_val=EXPERTS - 1)
                V.tensor_copy(b1_now[:, :], b1_sb[:, bass.ds(e, 1)])
                V.tensor_copy(w1_now[:, :], w1_sb[:, bass.ds(e, 1), :].rearrange("p a f -> p (a f)")).then_inc(s_w1, 1)
                with dve.Fori(0, QUADS // 2) as two:
                    q = two * 2
                    for i in range(2):
                        dve.wait_ge(s_e_mm, k * QUADS + q + i + 1)
                        for t in range(QUAD):
                            tile = (q + i) * QUAD + t
                            row = acc_all[:, bass.ds(tile, 1), :].rearrange("p a f -> p (a f)")
                            gate = gates[:, :, :].rearrange("p t e -> p (t e)")[:, bass.ds(tile * EXPERTS + e, 1)]
                            V.scalar_tensor_tensor(out=row, in0=bank_s[i][:, t, :], scalar=gate, in1=row,
                                                   op0=ALU.mult, op1=ALU.add).then_inc(s_e, 1)

        @block.sync
        def _(sp):
            for t, src in ((cond_sb[:, :], condT), (affw_sb[:, :, :], aff_wT), (affb_sb[:, :], aff_b),
                           (modb_sb[:, :], mod_b)):
                sp.dma_start(t, src).then_inc(s_ld_mod, 16)
            sp.dma_start(modw_sb[:, :, :], mod_wT).then_inc(s_ld_modw, 16)
            half = TOKENS // 2
            sp.dma_start(x_all[:, 0:QUAD * P], xT[:, 0:QUAD * P]).then_inc(s_ld_x0, 16)
            sp.dma_start(wk_sb[:, :], wk).then_inc(s_ld_qkv, 16)
            sp.dma_start(wv_sb[:, :], wv).then_inc(s_ld_qkv, 16)
            sp.dma_start(wq_sb[:, :], wq).then_inc(s_ld_qkv, 16)
            sp.dma_start(x_all[:, QUAD * P:half], xT[:, QUAD * P:half]).then_inc(s_ld_x, 16)
            sp.dma_start(x_all[:, half:TOKENS], xT[:, half:TOKENS]).then_inc(s_ld_x, 16)
            sp.dma_start(wpost_sb[:, :, :], wpost.rearrange("(c k) n -> k c n", k=P)).then_inc(s_ld_post, 16)
            sp.dma_start(gate_sb[:, :], gate_wT).then_inc(s_ld_post, 16)
            sp.dma_start(w1_sb[:, :, :], w1.rearrange("e h f -> h e f")).then_inc(s_ld_ffn, 16)
            sp.dma_start(w2_sb[:, :, :], w2.rearrange("e h f -> h e f")).then_inc(s_ld_ffn, 16)
            sp.dma_start(b1_sb[:, :], b1T).then_inc(s_ld_ffn, 16)
            sp.wait_ge(s_zero, 2)
            for i in range(P // EXPERTS):
                sp.dma_start(b2_rows[i * EXPERTS:(i + 1) * EXPERTS, i, :], b2).then_inc(s_ld_ffn, 16)
            sp.wait_ge(s_rt, ROUTE_STEPS["n"])
            before_last = sp.value_load(n_run[0:1, 1:2], min_val=1, max_val=EXPERTS - 1)
            for q in range(QUADS):
                sp.wait_ge(s_e, QUADS + before_last * (QUADS * QUAD) + (q + 1) * QUAD)
                sp.dma_start(out[q * QUAD * P:(q + 1) * QUAD * P, :].rearrange("(t p) c -> p t c", p=P),
                             acc_all[:, q * QUAD:(q + 1) * QUAD, :]).then_inc(s_out, 16)
            sp.wait_ge(s_out, 16 * QUADS)

        @block.tensor
        def _(pe):
            mm = nc.tensor.matmul

            pe.wait_ge(s_ld_mod, 64)
            for m in range(3):
                last = mm(misc[0][:, 0, m * BATCH:(m + 1) * BATCH], affw_sb[:, m, :], cond_sb[:, :],
                          start=(m == 0), stop=True, skip_group_check=True)
            last.then_inc(s_style_mm, 1)
            pe.wait_ge(s_sq, 2)
            for m in range(3):
                last = mm(misc[1][:, 0, m * BATCH:(m + 1) * BATCH], modw_sq[:, m, :], style_sq[:, m, :],
                          start=(m == 0), stop=True, skip_group_check=True)
            last.then_inc(s_power_mm, 1)
            pe.wait_ge(s_power, 1)
            pe.wait_ge(s_const, 3)
            pe.wait_ge(s_ld_qkv, 48)

            def scores(s, j, g):
                need(pe, s_max, 4 * s + g - 1)
                for i in range(2):
                    last = mm(bank_s[g % 2][:, 2 * i:2 * i + 2, :], q16[:, j, 2 * g + i, :],
                              k16[:, j, g, :, :], start=(i == 0), stop=True, skip_group_check=True)
                last.then_inc(s_s_mm, 1)

            def scores_t(s, j, g):
                need(pe, s_prob, 4 * s + g - 1)
                for par in range(2):
                    mm(bank_t[g % 2][:, par:HPG:2, :], k_pad[:, j, g, par, :],
                       qT[:, j, 2 * g:2 * g + 2, :], start=(par == 0), stop=False, skip_group_check=True)
                for w in range(HPG):
                    last = mm(bank_t[g % 2][:, w, :], pick[:, HPG * g + w, :], neg_max[:, :],
                              start=False, stop=True, skip_group_check=True)
                last.then_inc(s_t_mm, 1)

            def attend(s, j, g):
                pe.wait_ge(s_prob, 4 * s + g + 1)
                need(pe, s_att, 4 * s + g - 1)
                for w in range(HPG):
                    last = mm(att_bank(g)[:, w, :], prob[:, g % 2, w, :], v1[:, j, g, :],
                              start=(w == 0), stop=True, skip_group_check=True)
                last.then_inc(s_av_mm, 1)

            def queries(b, half):
                for c in range(4 * half, 4 * half + 4):
                    last = mm(misc[half][:, c % 4, :], wq_sb[:, c * P:(c + 1) * P], yT[:, :],
                              start=(c % 4 == 0), stop=True, skip_group_check=True)
                last.then_inc(s_q_mm, 1)

            def att_transpose(s, half):
                pe.wait_ge(s_att, 4 * s + 2 * half + 2)
                for c in range(4 * half, 4 * half + 4):
                    last = nc.tensor.transpose(misc[half][:, c % 4, :],
                                               att[:, 2 * c:2 * c + 2, :].rearrange("p h e -> p (h e)"),
                                               ident[:, :])
                last.then_inc(s_attT_mm, 1)

            def slot(s, j):
                a, c, d = s + 1, s - 1, s - 2
                A, B, C, D = has(a), has(s), has(c), has(d)
                ja, jd = 1 - j, j
                if A:
                    bank_free(pe, 0, s, "y")
                    pe.wait_ge(s_xs, n(a))
                    mm(misc[0][:, 0, :], modw_sb[:, 0, :], xs[:, ja, :], start=True, stop=True).then_inc(s_y_mm, 1)
                if B:
                    pe.wait_ge(s_q16, n(s))
                    pe.wait_ge(s_k16, n(s))
                    scores(s, j, 0)
                    scores(s, j, 1)
                if C:
                    if isinstance(s, int) and c == 0:
                        pe.wait_ge(s_ld_post, 32)
                    pe.wait_ge(s_attT, 2 * n(c))
                    for k in range(CHUNKS):
                        last = mm(misc[1][:, 0, :], wpost_sb[:, k, :], attT[:, k, :],
                                  start=(k == 0), stop=(k == CHUNKS - 1))
                    last.then_inc(s_post_mm, 1)
                if B:
                    scores(s, j, 2)
                    scores(s, j, 3)
                if A:
                    pe.wait_ge(s_yT, n(a))
                    queries(a, 0)
                if B:
                    bank_free(pe, 1, s, "neg")
                    pe.wait_ge(s_max, 4 * s + 4)
                    nc.tensor.transpose(misc[1][:, 0, :], row_max[:, :], ident[:, :]).then_inc(s_neg_mm, 1)
                if C:
                    bank_free(pe, 0, s, "kx")
                    pe.wait_ge(s_x1s, n(c))
                    mm(misc[0][:, 0, :], modw_sb[:, 1, :], x1s[:, :], start=True, stop=True).then_inc(s_kx_mm, 1)
                if A:
                    bank_free(pe, 1, s, "q1")
                    queries(a, 1)
                if B:
                    pe.wait_ge(s_neg, n(s))
                    scores_t(s, j, 0)
                if C:
                    pe.wait_ge(s_kxT, n(c))
                    nc.tensor.transpose(misc[0][:, 0, :], kxT[:, :], ident[:, :]).then_inc(s_kxn_mm, 1)
                if B:
                    scores_t(s, j, 1)
                if A:
                    bank_free(pe, 1, s, "kv")
                    for i in range(2):
                        mm(misc[1][:, i, :], wk_sb[:, i * P:(i + 1) * P], yT[:, :],
                           start=(i == 0), stop=True, skip_group_check=True)
                    mm(misc[1][:, 2:4, :].rearrange("p a f -> p (a f)"), yT[:, :], wv_sb[:, :], start=False,
                       stop=True, skip_group_check=True).then_inc(s_kv_mm, 1)
                if B:
                    attend(s, j, 0)
                    scores_t(s, j, 2)
                    attend(s, j, 1)
                if C:
                    bank_free(pe, 0, s, "x1n")
                    nc.tensor.transpose(misc[0][:, 0, :], x1T[:, :], ident[:, :]).then_inc(s_x1n_mm, 1)
                if B:
                    scores_t(s, j, 3)
                if D:
                    bank_free(pe, 1, s, "mix")
                    pe.wait_ge(s_mix, n(d))
                    nc.tensor.transpose(misc[1][:, 0, :], mix[:, :], ident[:, :]).then_inc(s_mixT_mm, 1)
                if B:
                    attend(s, j, 2)
                if D:
                    bank_free(pe, 0, s, "o")
                    pe.wait_ge(s_mixT, n(d))
                    mm(misc[0][:, 0, :], modw_sb[:, 2, :], mixT[:, :], start=True, stop=True).then_inc(s_o_mm, 1)
                if B:
                    attend(s, j, 3)
                if D:
                    pe.wait_ge(s_tok, n(d))
                    mm(misc[1][:, 0, 0:EXPERTS], tokT[:, :], gate_sb[:, :], start=True, stop=True).then_inc(s_log_mm, 1)
                if B:
                    bank_free(pe, 0, s, "att0")
                    att_transpose(s, 0)
                    bank_free(pe, 1, s, "att1")
                    att_transpose(s, 1)

            slots(pe, slot)

            pe.wait_ge(s_log, BATCH)
            pe.wait_ge(s_rt, ROUTE_STEPS["count"])
            mm(misc[0][:, 0, 0:EXPERTS], ones[:, :], count[:, :], start=True, stop=True).then_inc(s_cnt_mm, 1)
            pe.wait_ge(s_rt, ROUTE_STEPS["gates"])
            for i in range(2):
                src = gates[:, i * 16:(i + 1) * 16, :].rearrange("p t e -> p (t e)")
                last = nc.tensor.transpose(misc[1][:, i, :], src, ident[:, :])
            last.then_inc(s_gT_mm, 1)
            pe.wait_ge(s_gT, 1)
            pe.wait_ge(s_ld_ffn, 16 * (3 + P // EXPERTS))
            for q in range(QUADS):
                need(pe, s_e, q - 1)
                for t in range(QUAD):
                    i = q * QUAD + t
                    last = mm(bank_s[q % 2][:, t, :], gatesT[:, i // 16, :], b2_rows[:, i % 16, :],
                              start=(t == 0), stop=True, skip_group_check=True)
                last.then_inc(s_b2_mm, 1)
            pe.wait_ge(s_e, QUADS)
            pe.wait_ge(s_tok_kept, BATCH)
            pe.wait_ge(s_rt, ROUTE_STEPS["n"])
            runs = pe.value_load(n_run[0:1, 0:1], min_val=2, max_val=EXPERTS)

            with pe.Fori(0, runs) as k:
                e = pe.value_load(order[0:1, bass.ds(k, 1)], min_val=0, max_val=EXPERTS - 1)
                with pe.Fori(0, QUADS // 2) as two:
                    q = two * 2
                    for i in range(2):
                        pe.wait_ge(s_w1, k + 1)
                        mm(bank_t[i][:, :, :], w1_now[:, :], tok_all[:, bass.ds((q + i) * QUAD * P, QUAD * P)],
                           start=True, stop=True).then_inc(s_h_mm, 1)
                    for i in range(2):
                        pe.wait_ge(s_h, k * QUADS + q + i + 1)
                        pe.wait_ge(s_e, QUADS + (k * QUADS + q + i - 1) * QUAD)
                        for t in range(QUAD):
                            last = mm(bank_s[i][:, t, :], hT[:, i, t * P:(t + 1) * P],
                                      w2_sb[:, bass.ds(e, 1), :].rearrange("p a f -> p (a f)"),
                                      start=(t == 0), stop=True, skip_group_check=True)
                        last.then_inc(s_e_mm, 1)

        @block.scalar
        def _(act):
            def f(out_, in_, func=ACT.Copy, **kw):
                return nc.scalar.activation(out_, in_, func, **kw)

            act.wait_ge(s_ld_mod, 64)
            act.wait_ge(s_style_mm, 1)
            gains = (1.0 / COND ** 0.5, 1.0, 1.0)
            for m in range(3):
                f(style[:, m, :], misc[0][:, 0, m * BATCH:(m + 1) * BATCH], ACT.Identity,
                  bias=affb_sb[:, m:m + 1], scale=gains[m]).then_inc(s_style, 1)
            act.wait_ge(s_power, 1)
            f(root[:, :, :], power[:, :, :], ACT.Sqrt).then_inc(s_root, 1)
            act.wait_ge(s_demod, 5)
            act.wait_ge(s_zero, 5)

            def exp_scores(s, g):
                act.wait_ge(s_t_mm, 4 * s + g + 1)
                need(act, s_av_mm, 4 * s + g - 1)
                f(prob[:, g % 2, :, :], bank_t[g % 2][:, :, :], ACT.Exp, scale=KEY_SCALE).then_inc(s_prob, 1)

            def copy_q(b, j, half):
                act.wait_ge(s_q_mm, 2 * b + half + 1)
                need(act, s_t_mm, 4 * n(b - 2))
                need(act, s_q16, n(b - 2))
                f(qT[:, j, 4 * half:4 * half + 4, :], misc[half][:, :, :]).then_inc(s_q, 1)

            def slot(s, j):
                a, c, d = s + 1, s - 1, s - 2
                A, B, C, D = has(a), has(s), has(c), has(d)
                ja, jc, jd = 1 - j, 1 - j, j
                if A:
                    act.wait_ge(s_y_mm, n(a))
                    need(act, s_yT, n(a - 1))
                    act.wait_ge(s_demod, 5)
                    f(y_raw[:, :], misc[0][:, 0, :], ACT.Identity, scale=demod[:, 0, bass.ds(a, 1)],
                      bias=modb_sb[:, 0:1]).then_inc(s_y_raw, 1)
                if C:
                    act.wait_ge(s_x1T, n(c))
                    need(act, s_kx_mm, n(c - 1))
                    act.wait_ge(s_demod, 5)
                    f(x1s[:, :], x1T[:, :], scale=style[:, 1, bass.ds(c, 1)]).then_inc(s_x1s, 1)
                if A:
                    copy_q(a, ja, 0)
                if D:
                    act.wait_ge(s_shifted, n(d))
                    f(weight[:, jd, :, :], shifted[:, :, :], ACT.Exp, scale=MIX_SCALE).then_inc(s_weight, 1)
                if B:
                    act.wait_ge(s_neg_mm, n(s))
                    need(act, s_t_mm, 4 * n(s - 1))
                    f(neg_max[:, :], misc[1][:, 0, :], scale=-1.0).then_inc(s_neg, 1)
                if C:
                    act.wait_ge(s_kx_mm, n(c))
                    need(act, s_kxn_mm, n(c - 1))
                    act.wait_ge(s_demod, 5)
                    f(kxT[:, :], misc[0][:, 0, :], ACT.Identity, scale=demod[:, 1, bass.ds(c, 1)],
                      bias=modb_sb[:, 1:2]).then_inc(s_kxT, 1)
                if A:
                    copy_q(a, ja, 1)
                if B:
                    exp_scores(s, 0)
                if C:
                    act.wait_ge(s_kxn_mm, n(c))
                    need(act, s_lo, 4 * n(c - 2))
                    need(act, s_hi, 4 * n(c - 2))
                    f(kx2[:, jc, :].rearrange("p (r f) -> p r f", r=2),
                      misc[0][:, 0:1, :].to_broadcast([P, 2, P])).then_inc(s_kx2, 1)
                if B:
                    exp_scores(s, 1)
                if A:
                    act.wait_ge(s_kv_mm, n(a))
                    need(act, s_av_mm, 4 * n(a - 2))
                    f(v1[:, ja, :, 0:KEY],
                      misc[1][:, 2:4, :].rearrange("p a (g e) -> p (a g) e", e=KEY)).then_inc(s_v, 1)
                    need(act, s_t_mm, 4 * n(a - 2))
                    need(act, s_k16, n(a - 2))
                    for src in range(2):
                        for par in range(2):
                            f(k_pad[par * KEY:(par + 1) * KEY, ja, src:GROUPS:2, par, :],
                              misc[1][src * KEY:(src + 1) * KEY, 0:2, :]).then_inc(s_k, 1)
                if B:
                    exp_scores(s, 2)
                if A:
                    act.wait_ge(s_q, 2 * n(a))
                    need(act, s_s_mm, 4 * n(a - 2))
                    f(q16[:, ja, :, :], qT[:, ja, :, :]).then_inc(s_q16, 1)
                if C:
                    act.wait_ge(s_x1n_mm, n(c))
                    act.wait_ge(s_demod, 5)
                    f(acc_all[:, bass.ds(c, 1), :].rearrange("p a f -> p (a f)"),
                      misc[0][:, 0, :]).then_inc(s_x1n, 1)
                if B:
                    exp_scores(s, 3)
                if D:
                    act.wait_ge(s_mixT_mm, n(d))
                    need(act, s_o_mm, n(d - 1))
                    act.wait_ge(s_demod, 5)
                    f(mixT[:, :], misc[1][:, 0, :], scale=style[:, 2, bass.ds(d, 1)]).then_inc(s_mixT, 1)
                    act.wait_ge(s_o_mm, n(d))
                    need(act, s_log_mm, n(d - 1))
                    need(act, s_tok_kept, n(d - 1))
                    act.wait_ge(s_demod, 5)
                    f(tokT[:, :], misc[0][:, 0, :], ACT.Identity, scale=demod[:, 2, bass.ds(d, 1)],
                      bias=modb_sb[:, 2:3]).then_inc(s_tok, 1)
                    act.wait_ge(s_log_mm, n(d))
                    act.wait_ge(s_demod, 5)
                    f(logits[:, bass.ds(d, 1), :].rearrange("p a e -> p (a e)"),
                      misc[1][:, 0, 0:EXPERTS]).then_inc(s_log, 1)
                if A:
                    act.wait_ge(s_k, 4 * n(a))
                    f(k16[:, ja, :, :, :], k_pad[:, ja, :, :, :]).then_inc(s_k16, 1)
                if B:
                    need(act, s_post_mm, n(s - 1))
                    for half in range(2):
                        act.wait_ge(s_attT_mm, 2 * s + half + 1)
                        f(attT[:, 4 * half:4 * half + 4, :], misc[half][:, :, :]).then_inc(s_attT, 1)

            slots(act, slot)

            act.wait_ge(s_rt, ROUTE_STEPS["exp"])
            f(gates[:, :, :], rest[:, :, :], ACT.Exp).then_inc(s_rt_exp, 1)
            act.wait_ge(s_gT_mm, 1)
            f(gatesT[:, :, :], misc[1][:, 0:2, :]).then_inc(s_gT, 1)
            act.wait_ge(s_ld_ffn, 16 * (3 + P // EXPERTS))
            act.wait_ge(s_rt, ROUTE_STEPS["n"])
            runs = act.value_load(n_run[0:1, 0:1], min_val=2, max_val=EXPERTS)
            with act.Fori(0, runs) as k:
                with act.Fori(0, QUADS // 2) as two:
                    q = two * 2
                    for i in range(2):
                        act.wait_ge(s_h_mm, k * QUADS + q + i + 1)
                        f(hT[:, i, :], bank_t[i][:, :, :].rearrange("p t f -> p (t f)"), ACT.Relu,
                          bias=b1_now[:, :]).then_inc(s_h, 1)

        @block.gpsimd
        def _(pool):
            G = nc.gpsimd
            G.memset(ident[:, :], 0.0).then_inc(s_blank, 1)
            G.memset(pick[:, :, :], 0.0).then_inc(s_blank, 1)
            G.memset(before[:, :, :], 0.0).then_inc(s_const, 1)
            pool.wait_ge(s_blank, 2)
            pool.wait_ge(s_const, 1)
            G.affine_select(out=ident[:, :], in_=ident[:, :], compare_op=ALU.not_equal, fill=1.0, base=0,
                            pattern=[[-1, P]], channel_multiplier=1).then_inc(s_const, 1)
            G.affine_select(out=pick[:, :, :], in_=pick[:, :, :], compare_op=ALU.not_equal, fill=1.0, base=0,
                            pattern=[[-1, HEADS], [0, P]], channel_multiplier=1).then_inc(s_const, 1)

            pool.wait_ge(s_style, 3)

            def slot(s, j):
                a, c, d = s + 1, s - 1, s - 2
                A, B, C, D = has(a), has(s), has(c), has(d)
                ja, jc, jd = 1 - j, 1 - j, j

                def xs_of(b, jb):
                    need(pool, s_y_mm, n(b - 2))
                    pool.wait_ge(s_style, 3)
                    G.tensor_tensor(xs[:, jb, :], x_all[:, col(b)],
                                    style[:, 0, bass.ds(b, 1)].to_broadcast([P, P]), ALU.mult).then_inc(s_xs, 1)

                if isinstance(s, int) and s == -1:
                    pool.wait_ge(s_ld_x0, 16)
                    xs_of(0, 0)
                if isinstance(s, int) and s == LOOP_FROM - 1:
                    pool.wait_ge(s_ld_x, 32)
                if has(s + 2):
                    xs_of(s + 2, j)
                if D:
                    pool.wait_ge(s_weight, n(d))
                    need(pool, s_msum, n(d - 1))
                    G.tensor_tensor(mix_hi[:, :, :].rearrange("p r (h e) -> p r h e", e=MD),
                                    weight[:, jd, MH // 2:MH, :].unsqueeze(3).to_broadcast([P, MH // 2, MH, MD]),
                                    bass.AP(kx2, jd * 2 * P + MD * MH // 2,
                                            [[4 * P, P], [MD, MH // 2], [MD, MH], [1, MD]]),
                                    ALU.mult).then_inc(s_hi, 1)
                    for i, r in enumerate((4, 2, 1)):
                        pool.wait_ge(s_hi, 4 * d + i + 1)
                        G.tensor_tensor(mix_hi[:, 0:r, :], mix_hi[:, 0:r, :], mix_hi[:, r:2 * r, :],
                                        ALU.add).then_inc(s_hi, 1)
                if C:
                    pool.wait_ge(s_kx2, n(c))
                    need(pool, s_score, n(c - 1))
                    G.tensor_tensor(pair[:, :, :],
                                    bass.AP(kx2, jc * 2 * P, [[4 * P, P], [0, SHIFTS], [1, P]]),
                                    bass.AP(kx2, jc * 2 * P, [[4 * P, P], [MD, SHIFTS], [1, P]]),
                                    ALU.mult).then_inc(s_pair, 1)
                if D:
                    pool.wait_ge(s_tok, n(d))
                    pool.wait_ge(s_ld_x0, 16)
                    G.tensor_copy(tok_all[:, col(d)], tokT[:, :]).then_inc(s_tok_kept, 1)
                if isinstance(s, int) and s == 0:
                    for e in range(EXPERTS):
                        G.memset(index8[:, e:e + 1], float(e))
                        last = G.memset(rank8[:, e:e + 1], float(EXPERTS - e))
                        if e:
                            last = G.memset(before[:, e, 0:e], 1.0)
                    last.then_inc(s_const, 1)

            slots(pool, slot)


_INS = ("xT", "condT", "aff_wT", "aff_b", "mod_wT", "mod_b", "wq", "wk", "wv", "wpost", "gate_wT",
        "w1", "b1T", "w2", "b2")


def kernel(x, cond_512, L0_cond_weight, L0_cond_bias, L0_cond_affine_w, L0_cond_affine_b, L0_attn_Wq,
           L0_attn_Wk, L0_attn_Wv, L0_attn_Wpost, L0_cond2_k_aff_w, L0_cond2_k_aff_b, L0_cond2_k_w,
           L0_cond2_k_b, L0_cond2_o_aff_w, L0_cond2_o_aff_b, L0_cond2_o_w, L0_cond2_o_b, L0_ffn_gate_w,
           L0_ffn_W1, L0_ffn_b1, L0_ffn_W2, L0_ffn_b2):
    import concourse.bacc as bacc
    from concourse.bass_utils import run_bass_kernel_spmd

    arrays = {
        "xT": np.asarray(x).reshape(TOKENS, P).T,
        "condT": np.asarray(cond_512).T,
        "aff_wT": np.stack([np.asarray(w).T for w in (L0_cond_affine_w, L0_cond2_k_aff_w, L0_cond2_o_aff_w)], 1),
        "aff_b": np.stack([np.asarray(w) for w in (L0_cond_affine_b, L0_cond2_k_aff_b, L0_cond2_o_aff_b)], 1),
        "mod_wT": np.stack([np.asarray(w).T for w in (L0_cond_weight, L0_cond2_k_w, L0_cond2_o_w)], 1),
        "mod_b": np.stack([np.asarray(w) for w in (L0_cond_bias, L0_cond2_k_b, L0_cond2_o_b)], 1),
        "wq": L0_attn_Wq, "wk": L0_attn_Wk, "wv": L0_attn_Wv, "wpost": L0_attn_Wpost,
        "gate_wT": np.asarray(L0_ffn_gate_w).T,
        "w1": L0_ffn_W1, "b1T": np.asarray(L0_ffn_b1).T, "w2": L0_ffn_W2, "b2": L0_ffn_b2,
    }
    arrays = {k: np.ascontiguousarray(v) for k, v in arrays.items()}
    nc = bacc.Bacc("TRN2", target_bir_lowering=False, num_devices=1)
    ins = [nc.dram_tensor(f"in_{k}", arrays[k].shape, mybir.dt.from_np(arrays[k].dtype),
                          kind="ExternalInput").ap() for k in _INS]
    out = nc.dram_tensor("out", (TOKENS, P), F32, kind="ExternalOutput").ap()
    build(nc, *ins, out)
    result = run_bass_kernel_spmd(nc, [{f"in_{k}": arrays[k] for k in _INS}], core_ids=[0])
    return result.results[0]["out"].reshape(BATCH, P, P)
```

```python
from contextlib import ExitStack

import numpy as np

import concourse.bass as bass
from concourse import mybir

F32 = mybir.dt.float32
BF16 = mybir.dt.bfloat16
I32 = mybir.dt.int32
ALU = mybir.AluOpType
ACT = mybir.ActivationFunctionType
AX = mybir.AxisListType

P = 128
BATCH = 32
TOKENS = BATCH * P
COND = 64
GROUPS, HPG, KEY = 4, 4, 64
HEADS = GROUPS * HPG
CHUNKS = HEADS * KEY // P
MH, MD = 16, 8
SHIFTS = MH // 2 + 1
EXPERTS = 8
CAP = int(1.25 * TOKENS / EXPERTS)
QUAD = 4
QUADS = BATCH // QUAD
CLAMP = 256.0
EPS = 1e-8
KEY_SCALE = 1.0 / KEY ** 0.5
MIX_SCALE = 1.0 / MD ** 0.5
LOOP_FROM, LOOP_TO = 4, BATCH - 2


def build(nc, xT, condT, aff_wT, aff_b, mod_wT, mod_b, wq, wk, wv, wpost, gate_wT,
          w1, b1T, w2, b2, out):
    ctx = ExitStack()
    with ctx:
        def sb(name, shape, dt=F32):
            return ctx.enter_context(nc.sbuf_tensor(name, shape, dt))

        def pb(name, shape, dt=F32):
            return ctx.enter_context(nc.psum_tensor(name, shape, dt))

        def sem(name):
            return ctx.enter_context(nc.semaphore(name))

        x_all = sb("x_all", [P, TOKENS])
        tok_all = sb("tok_all", [P, TOKENS])
        acc_all = sb("acc_all", [P, BATCH, P])
        logits = sb("logits", [P, BATCH, EXPERTS])
        ident = sb("ident", [P, P])
        ones = sb("ones", [P, P])
        pick = sb("pick", [P, HEADS, P], BF16)
        cond_sb = sb("cond_sb", [COND, BATCH])
        affw_sb = sb("affw_sb", [COND, 3, P])
        affb_sb = sb("affb_sb", [P, 3])
        modw_sb = sb("modw_sb", [P, 3, P])
        modb_sb = sb("modb_sb", [P, 3])
        wq_sb = sb("wq_sb", [P, HEADS * KEY])
        wk_sb = sb("wk_sb", [P, GROUPS * KEY])
        wv_sb = sb("wv_sb", [P, GROUPS * KEY])
        wpost_sb = sb("wpost_sb", [P, CHUNKS, P])
        gate_sb = sb("gate_sb", [P, EXPERTS])
        w1_sb = sb("w1_sb", [P, EXPERTS, P])
        w2_sb = sb("w2_sb", [P, EXPERTS, P])
        b1_sb = sb("b1_sb", [P, EXPERTS])
        b2_rows = sb("b2_rows", [P, P // EXPERTS, P])
        style = sb("style", [P, 3, BATCH])
        demod = sb("demod", [P, 3, BATCH])
        style_sq = sb("style_sq", [P, 3, BATCH])
        modw_sq = sb("modw_sq", [P, 3, P])
        power = sb("power", [P, 3, BATCH])
        root = sb("root", [P, 3, BATCH])
        inv_root = sb("inv_root", [P, 3, BATCH])
        newton = sb("newton", [P, 3, BATCH])
        xs = sb("xs", [P, 2, P])
        y_raw = sb("y_raw", [P, P])
        yT = sb("yT", [P, P])
        qT = sb("qT", [P, 2, CHUNKS, P])
        q16 = sb("q16", [P, 2, CHUNKS, P], BF16)
        k_pad = sb("k_pad", [P, 2, GROUPS, 2, P])
        k16 = sb("k16", [P, 2, GROUPS, 2, P], BF16)
        v1 = sb("v1", [P, 2, GROUPS, KEY + 1])
        row_max = sb("row_max", [P, P])
        neg_max = sb("neg_max", [P, P], BF16)
        prob = sb("prob", [P, 2, HPG, P])
        recip_den = sb("recip_den", [P, 2, HPG])
        att = sb("att", [P, HEADS, KEY])
        attT = sb("attT", [P, CHUNKS, P])
        x1T = sb("x1T", [P, P])
        x1s = sb("x1s", [P, P])
        kxT = sb("kxT", [P, P])
        kx2 = sb("kx2", [P, 2, 2 * P])
        pair = sb("pair", [P, SHIFTS, P])
        score = sb("score", [P, MH, 2 * MH])
        h_max = sb("h_max", [P, MH])
        shifted = sb("shifted", [P, MH, MH])
        weight = sb("weight", [P, 2, MH, MH])
        h_den = sb("h_den", [P, MH])
        h_rden = sb("h_rden", [P, MH])
        mix_lo = sb("mix_lo", [P, MH // 2, P])
        mix_hi = sb("mix_hi", [P, MH // 2, P])
        mix_sum = sb("mix_sum", [P, P])
        mix = sb("mix", [P, P])
        mixT = sb("mixT", [P, P])
        tokT = sb("tokT", [P, P])
        r_max = sb("r_max", [P, BATCH])
        r_key = sb("r_key", [P, BATCH])
        gates = sb("gates", [P, BATCH, EXPERTS])
        rest = sb("rest", [P, BATCH, EXPERTS])
        cand = sb("cand", [P, BATCH, EXPERTS])
        first = sb("first", [P, BATCH, EXPERTS])
        chosen = sb("chosen", [P, BATCH, EXPERTS])
        rank8 = sb("rank8", [P, EXPERTS])
        index8 = sb("index8", [P, EXPERTS])
        before = sb("before", [P, EXPERTS, EXPERTS])
        count = sb("count", [P, EXPERTS])
        keep = sb("keep", [P, EXPERTS])
        t88 = sb("t88", [P, EXPERTS, EXPERTS])
        place = sb("place", [P, EXPERTS])
        drop_place = sb("drop_place", [P, EXPERTS])
        kept = sb("kept", [P, 1])
        order_f = sb("order_f", [P, EXPERTS])
        order = sb("order", [P, EXPERTS], I32)
        n_run = sb("n_run", [P, 2], I32)
        gatesT = sb("gatesT", [P, 2, P])
        w1_now = sb("w1_now", [P, P])
        b1_now = sb("b1_now", [P, 1])
        hT = sb("hT", [P, 2, QUAD * P])

        bank_s = pb("bank_s", [P, HPG, P])
        bank_t = [pb(f"bank_t{i}", [P, HPG, P]) for i in range(2)]
        bank_a = [pb(f"bank_a{i}", [P, 512]) for i in range(2)]
        misc = [pb(f"misc{i}", [P, QUAD, P]) for i in range(3)]
        bank_e = [bank_s, misc[2]]

        def att_bank(g):
            return bank_a[g % 2][:, 0:HPG * (KEY + 1)].rearrange("p (w e) -> p w e", e=KEY + 1)

        s_ld_mod, s_ld_modw, s_ld_x0, s_ld_x, s_ld_qkv = (sem("ld_mod"), sem("ld_modw"), sem("ld_x0"),
                                                         sem("ld_x"), sem("ld_qkv"))
        s_ld_post, s_ld_ffn = sem("ld_post"), sem("ld_ffn")
        s_out = sem("out_written")
        s_const, s_blank, s_zero = sem("const"), sem("blank"), sem("zero")
        s_style_mm, s_style, s_sq, s_power_mm = sem("style_mm"), sem("style"), sem("sq"), sem("power_mm")
        s_power, s_root, s_demod = sem("power"), sem("root"), sem("demod")
        s_xs, s_y_mm, s_y_raw, s_yT, s_xy = sem("xs"), sem("y_mm"), sem("y_raw"), sem("yT"), sem("xy")
        s_q_mm, s_q, s_kv_mm, s_k, s_v = sem("q_mm"), sem("q"), sem("kv_mm"), sem("k"), sem("v")
        s_q16, s_k16 = sem("q16"), sem("k16")
        s_s_mm, s_max, s_t_mm, s_prob = sem("s_mm"), sem("max"), sem("t_mm"), sem("prob")
        s_av_mm, s_rden, s_att = sem("av_mm"), sem("rden"), sem("att")
        s_neg_mm, s_neg = sem("neg_mm"), sem("neg")
        s_attT_mm, s_attT = sem("attT_mm"), sem("attT")
        s_post_mm, s_x1T, s_x1s, s_kx_mm, s_kxT = sem("post_mm"), sem("x1T"), sem("x1s"), sem("kx_mm"), sem("kxT")
        s_kxn_mm, s_kx2, s_x1n_mm, s_x1n = sem("kxn_mm"), sem("kx2"), sem("x1n_mm"), sem("x1n")
        s_pair, s_score, s_twice, s_mirror = sem("pair"), sem("score"), sem("twice"), sem("mirror")
        s_hmax, s_shifted, s_weight = sem("hmax"), sem("shifted"), sem("weight")
        s_hden, s_hrden, s_lo, s_hi = sem("hden"), sem("hrden"), sem("lo"), sem("hi")
        s_msum, s_mix, s_mixT_mm, s_mixT = sem("msum"), sem("mix"), sem("mixT_mm"), sem("mixT")
        s_o_mm, s_tok, s_tok_kept, s_log_mm, s_log = (sem("o_mm"), sem("tok"), sem("tok_kept"),
                                                      sem("log_mm"), sem("log"))
        s_rt, s_rt_exp, s_cnt_mm, s_gT_mm, s_gT = sem("rt"), sem("rt_exp"), sem("cnt_mm"), sem("gT_mm"), sem("gT")
        s_b2_mm = sem("b2_mm")
        s_w1, s_h_mm, s_h, s_e_mm = sem("w1"), sem("h_mm"), sem("h"), sem("e_mm")
        s_e = sem("e")

        ROUTE_STEPS = {}

        def n(b):
            return b + 1

        def need(eng, s, v):
            if not (isinstance(v, int) and v <= 0):
                eng.wait_ge(s, v)

        def has(b):
            return not isinstance(b, int) or 0 <= b < BATCH

        def bank_users(bank, s):
            a, c, h, d = s + 1, s - 1, s - 2, s - 3
            return ((("q0", a, [(s_q, 2 * a + 1)]), ("q1", a, [(s_q, 2 * a + 2)]),
                     ("kv", a, [(s_v, n(a)), (s_k, 4 * n(a))]), ("y", a + 1, [(s_y_raw, n(a + 1))])),
                    (("att0", c, [(s_attT, 2 * c + 1)]), ("neg", s, [(s_neg, n(s))]), ("kx", c, [(s_kxT, n(c))]),
                     ("kxn", c, [(s_kx2, n(c))]), ("o", d, [(s_tok, n(d))])),
                    (("att1", c, [(s_attT, 2 * c + 2)]), ("post", c, [(s_x1T, n(c))]), ("mix", d, [(s_mixT, n(d))]),
                     ("x1n", c, [(s_x1n, n(c))]), ("log", d, [(s_log, n(d))])))[bank]

        def bank_free(eng, bank, s, use):
            now = bank_users(bank, s)
            at = [u[0] for u in now].index(use)
            for _, b, readers in (*reversed(now[:at]), *reversed(bank_users(bank, s - 1))):
                if has(b):
                    for sm, v in readers:
                        eng.wait_ge(sm, v)
                    return

        def slots(eng, slot):
            for s in range(-2, LOOP_FROM):
                slot(s, s % 2)
            with eng.Fori(LOOP_FROM // 2, LOOP_TO // 2) as two:
                slot(two * 2, 0)
                slot(two * 2 + 1, 1)
            for s in range(LOOP_TO, BATCH + 3):
                slot(s, s % 2)

        def col(b):
            return bass.ds(b * P, P)

        block = ctx.enter_context(nc.Block())

        @block.vector
        def _(dve):
            V = nc.vector
            V.memset(ones[:, :], 1.0).then_inc(s_zero, 1)
            V.memset(b2_rows[:, :, :], 0.0).then_inc(s_zero, 1)
            V.memset(k_pad[:, :, :, :, :], 0.0).then_inc(s_zero, 1)
            V.memset(v1[:, :, :, :], 1.0).then_inc(s_zero, 1)
            V.memset(row_max[:, :], 0.0).then_inc(s_zero, 1)

            dve.wait_ge(s_ld_modw, 16)
            V.tensor_tensor(modw_sq[:, :, :], modw_sb[:, :, :], modw_sb[:, :, :], ALU.mult).then_inc(s_sq, 1)
            dve.wait_ge(s_style, 3)
            V.tensor_tensor(style_sq[:, :, :], style[:, :, :], style[:, :, :], ALU.mult).then_inc(s_sq, 1)
            dve.wait_ge(s_power_mm, 1)
            V.tensor_scalar(power[:, :, :], misc[1][:, 0, 0:3 * BATCH].rearrange("p (m b) -> p m b", m=3),
                            EPS, None, ALU.add).then_inc(s_power, 1)
            dve.wait_ge(s_root, 1)
            V.reciprocal(inv_root[:, :, :], root[:, :, :]).then_inc(s_demod, 1)
            dve.wait_ge(s_demod, 1)
            V.tensor_tensor(newton[:, :, :], inv_root[:, :, :], inv_root[:, :, :], ALU.mult).then_inc(s_demod, 1)
            dve.wait_ge(s_demod, 2)
            V.tensor_tensor(newton[:, :, :], newton[:, :, :], power[:, :, :], ALU.mult).then_inc(s_demod, 1)
            dve.wait_ge(s_demod, 3)
            V.tensor_scalar(newton[:, :, :], newton[:, :, :], -0.5, 1.5, ALU.mult, ALU.add).then_inc(s_demod, 1)
            dve.wait_ge(s_demod, 4)
            V.tensor_tensor(demod[:, :, :], newton[:, :, :], inv_root[:, :, :], ALU.mult).then_inc(s_demod, 1)
            dve.wait_ge(s_zero, 5)

            def group_max(s, g):
                dve.wait_ge(s_s_mm, 4 * s + g + 1)
                need(dve, s_neg_mm, n(s - 1))
                V.tensor_reduce(row_max[:, HPG * g:HPG * (g + 1)], bank_s[:, :, :], AX.X,
                                ALU.max).then_inc(s_max, 1)

            def invert(s, g):
                dve.wait_ge(s_av_mm, 4 * s + g + 1)
                need(dve, s_att, 4 * s + g - 1)
                V.reciprocal(recip_den[:, g % 2, :].unsqueeze(2), att_bank(g)[:, :, KEY:KEY + 1]).then_inc(s_rden, 1)

            def normalise(s, g):
                need(dve, s_attT_mm, 2 * n(s - 1))
                dve.wait_ge(s_rden, 4 * s + g + 1)
                V.tensor_tensor(att[:, HPG * g:HPG * (g + 1), :], att_bank(g)[:, :, 0:KEY],
                                recip_den[:, g % 2, :].unsqueeze(2).to_broadcast([P, HPG, KEY]),
                                ALU.mult).then_inc(s_att, 1)

            def slot(s, j):
                a, c, h, d = s + 1, s - 1, s - 2, s - 3
                A, B, C, H, D = has(a), has(s), has(c), has(h), has(d)
                ja, jc, jh, jd = 1 - j, 1 - j, j, 1 - j
                if B:
                    group_max(s, 3)
                if A:
                    dve.wait_ge(s_yT, n(a))
                    V.tensor_tensor(x_all[:, col(a)], x_all[:, col(a)], yT[:, :], ALU.add).then_inc(s_xy, 1)
                if D:
                    dve.wait_ge(s_weight, n(d))
                    need(dve, s_mix, n(d - 1))
                    V.tensor_tensor(mix_lo[:, :, :].rearrange("p r (h e) -> p r h e", e=MD),
                                    weight[:, jd, 0:MH // 2, :].unsqueeze(3).to_broadcast([P, MH // 2, MH, MD]),
                                    bass.AP(kx2, jd * 2 * P, [[4 * P, P], [MD, MH // 2], [MD, MH], [1, MD]]),
                                    ALU.mult).then_inc(s_lo, 1)
                if D:
                    V.tensor_reduce(h_den[:, :], weight[:, jd, :, :].rearrange("p r h -> p h r"), AX.X,
                                    ALU.add).then_inc(s_hden, 1)
                    dve.wait_ge(s_lo, 4 * d + 1)
                    V.tensor_tensor(mix_lo[:, 0:4, :], mix_lo[:, 0:4, :], mix_lo[:, 4:8, :], ALU.add).then_inc(s_lo, 1)
                if C:
                    dve.wait_ge(s_post_mm, n(c))
                    dve.wait_ge(s_xy, n(c))
                    need(dve, s_x1n_mm, n(c - 1))
                    need(dve, s_x1s, n(c - 1))
                    V.tensor_tensor(x1T[:, :], misc[2][:, 0, :], x_all[:, col(c)], ALU.add).then_inc(s_x1T, 1)
                if D:
                    dve.wait_ge(s_hden, n(d))
                    V.reciprocal(h_rden[:, :], h_den[:, :]).then_inc(s_hrden, 1)
                    dve.wait_ge(s_lo, 4 * d + 2)
                    V.tensor_tensor(mix_lo[:, 0:2, :], mix_lo[:, 0:2, :], mix_lo[:, 2:4, :], ALU.add).then_inc(s_lo, 1)
                    dve.wait_ge(s_lo, 4 * d + 3)
                    V.tensor_tensor(mix_lo[:, 0, :], mix_lo[:, 0, :], mix_lo[:, 1, :], ALU.add).then_inc(s_lo, 1)
                if D:
                    dve.wait_ge(s_lo, 4 * d + 4)
                    dve.wait_ge(s_hi, 4 * d + 4)
                    V.tensor_tensor(mix_sum[:, :], mix_lo[:, 0, :], mix_hi[:, 0, :], ALU.add).then_inc(s_msum, 1)
                    dve.wait_ge(s_hrden, n(d))
                    dve.wait_ge(s_msum, n(d))
                    need(dve, s_mixT_mm, n(d - 1))
                    V.tensor_tensor(mix[:, :].rearrange("p (h e) -> p h e", e=MD),
                                    mix_sum[:, :].rearrange("p (h e) -> p h e", e=MD),
                                    h_rden[:, :].unsqueeze(2).to_broadcast([P, MH, MD]), ALU.mult).then_inc(s_mix, 1)
                if H:
                    dve.wait_ge(s_pair, n(h))
                    need(dve, s_shifted, n(h - 1))
                    V.tensor_reduce(score[:, 0:SHIFTS, 0:MH], pair[:, :, :].rearrange("p r (h e) -> p r h e", e=MD),
                                    AX.X, ALU.add).then_inc(s_score, 1)
                if H:
                    dve.wait_ge(s_score, n(h))
                    V.tensor_copy(score[:, 1:MH // 2, MH:2 * MH], score[:, 1:MH // 2, 0:MH]).then_inc(s_twice, 1)
                if H:
                    dve.wait_ge(s_twice, n(h))
                    top = MH // 2 - 1
                    V.tensor_copy(score[:, SHIFTS:MH, 0:MH],
                                  bass.AP(score, top * (2 * MH - 1) + MH,
                                          [[2 * MH * MH, P], [-(2 * MH - 1), top], [1, MH]])).then_inc(s_mirror, 1)
                if H:
                    dve.wait_ge(s_mirror, n(h))
                    V.tensor_reduce(h_max[:, :], score[:, :, 0:MH].rearrange("p r h -> p h r"), AX.X,
                                    ALU.max).then_inc(s_hmax, 1)
                if H:
                    dve.wait_ge(s_hmax, n(h))
                    need(dve, s_weight, n(h - 1))
                    V.tensor_tensor(shifted[:, :, :], score[:, :, 0:MH],
                                    h_max[:, :].unsqueeze(1).to_broadcast([P, MH, MH]),
                                    ALU.subtract).then_inc(s_shifted, 1)
                if A:
                    dve.wait_ge(s_k, 4 * n(a))
                    need(dve, s_s_mm, 4 * n(a - 2))
                    V.tensor_copy(k16[:, ja, :, :, :], k_pad[:, ja, :, :, :]).then_inc(s_k16, 1)
                if B:
                    invert(s, 0)
                if B:
                    normalise(s, 0)
                if B:
                    invert(s, 1)
                if A:
                    group_max(a, 0)
                if B:
                    normalise(s, 1)
                if A:
                    group_max(a, 1)
                if B:
                    invert(s, 2)
                if A:
                    group_max(a, 2)
                if B:
                    normalise(s, 2)
                if has(a + 1):
                    dve.wait_ge(s_y_raw, n(a + 1))
                    need(dve, s_kv_mm, n(a))
                    need(dve, s_xy, n(a))
                    V.tensor_scalar(yT[:, :], y_raw[:, :], CLAMP, -CLAMP, ALU.min, ALU.max).then_inc(s_yT, 1)
                if B:
                    invert(s, 3)
                if B:
                    normalise(s, 3)

            slots(dve, slot)

            steps = [0]

            def step(ins):
                steps[0] += 1
                ins.then_inc(s_rt, 1)
                dve.wait_ge(s_rt, steps[0])
                return steps[0]

            def over_e(t):
                return t[:, :].unsqueeze(2).to_broadcast([P, BATCH, EXPERTS])

            def over_t(t):
                return t[:, :].unsqueeze(1).to_broadcast([P, BATCH, EXPERTS])

            dve.wait_ge(s_log, BATCH)
            step(V.tensor_reduce(r_max[:, :], logits[:, :, :], AX.X, ALU.max))
            ROUTE_STEPS["exp"] = step(V.tensor_tensor(rest[:, :, :], logits[:, :, :], over_e(r_max), ALU.subtract))
            dve.wait_ge(s_rt_exp, 1)
            step(V.tensor_reduce(r_key[:, :], gates[:, :, :], AX.X, ALU.add))
            step(V.reciprocal(r_max[:, :], r_key[:, :]))
            step(V.tensor_tensor(gates[:, :, :], gates[:, :, :], over_e(r_max), ALU.mult))

            def choose(src, dst):
                step(V.tensor_reduce(r_max[:, :], src[:, :, :], AX.X, ALU.max))
                step(V.tensor_tensor(cand[:, :, :], src[:, :, :], over_e(r_max), ALU.is_equal))
                step(V.tensor_tensor(cand[:, :, :], cand[:, :, :], over_t(rank8), ALU.mult))
                step(V.tensor_reduce(r_key[:, :], cand[:, :, :], AX.X, ALU.max))
                step(V.tensor_tensor(dst[:, :, :], over_t(rank8), over_e(r_key), ALU.is_equal))

            dve.wait_ge(s_const, 4)
            choose(gates, first)
            step(V.scalar_tensor_tensor(out=rest[:, :, :], in0=first[:, :, :], scalar=-2.0, in1=gates[:, :, :],
                                        op0=ALU.mult, op1=ALU.add))
            choose(rest, chosen)
            step(V.tensor_tensor(chosen[:, :, :], chosen[:, :, :], first[:, :, :], ALU.add))
            ROUTE_STEPS["count"] = step(V.tensor_reduce(count[:, :], chosen[:, :, :].rearrange("p t e -> p e t"),
                                                        AX.X, ALU.add))
            step(V.tensor_tensor(gates[:, :, :], gates[:, :, :], chosen[:, :, :], ALU.mult))
            dve.wait_ge(s_cnt_mm, 1)
            step(V.tensor_scalar(keep[:, :], misc[0][:, 0, 0:EXPERTS], float(CAP), None, ALU.is_le))
            ROUTE_STEPS["gates"] = step(V.tensor_tensor(gates[:, :, :], gates[:, :, :], over_t(keep), ALU.mult))
            wide = [P, EXPERTS, EXPERTS]
            step(V.tensor_tensor(t88[:, :, :], before[:, :, :], keep[:, :].unsqueeze(1).to_broadcast(wide), ALU.mult))
            step(V.tensor_reduce(place[:, :], t88[:, :, :], AX.X, ALU.add))
            step(V.tensor_reduce(kept[:, :], keep[:, :], AX.X, ALU.add))
            step(V.tensor_tensor(drop_place[:, :], index8[:, :], place[:, :], ALU.subtract))
            step(V.tensor_scalar(drop_place[:, :], drop_place[:, :], kept[:, 0:1], None, ALU.add))
            step(V.tensor_tensor(place[:, :], place[:, :], drop_place[:, :], ALU.subtract))
            step(V.tensor_tensor(place[:, :], place[:, :], keep[:, :], ALU.mult))
            step(V.tensor_tensor(place[:, :], place[:, :], drop_place[:, :], ALU.add))
            step(V.tensor_tensor(t88[:, :, :], index8[:, :].unsqueeze(2).to_broadcast(wide),
                                 place[:, :].unsqueeze(1).to_broadcast(wide), ALU.is_equal))
            step(V.tensor_tensor(t88[:, :, :], t88[:, :, :], index8[:, :].unsqueeze(1).to_broadcast(wide), ALU.mult))
            step(V.tensor_reduce(order_f[:, :], t88[:, :, :], AX.X, ALU.add))
            step(V.tensor_copy(order[:, :], order_f[:, :]))
            step(V.tensor_scalar(n_run[:, 0:1], kept[:, :], 2.0, None, ALU.max))
            ROUTE_STEPS["n"] = step(V.tensor_scalar(n_run[:, 1:2], kept[:, :], -1.0, 1.0, ALU.add, ALU.max))

            for q in range(QUADS):
                dve.wait_ge(s_b2_mm, q + 1)
                t = acc_all[:, q * QUAD:(q + 1) * QUAD, :]
                V.tensor_tensor(t, t, bank_e[q % 2][:, :, :], ALU.add).then_inc(s_e, 1)
            dve.wait_ge(s_ld_ffn, 16 * (3 + P // EXPERTS))
            runs = dve.value_load(n_run[0:1, 0:1], min_val=2, max_val=EXPERTS)
            with dve.Fori(0, runs) as k:
                e = dve.value_load(order[0:1, bass.ds(k, 1)], min_val=0, max_val=EXPERTS - 1)
                V.tensor_copy(b1_now[:, :], b1_sb[:, bass.ds(e, 1)])
                V.tensor_copy(w1_now[:, :], w1_sb[:, bass.ds(e, 1), :].rearrange("p a f -> p (a f)")).then_inc(s_w1, 1)
                with dve.Fori(0, QUADS // 2) as two:
                    q = two * 2
                    for i in range(2):
                        dve.wait_ge(s_e_mm, k * QUADS + q + i + 1)
                        for t in range(QUAD):
                            tile = (q + i) * QUAD + t
                            row = acc_all[:, bass.ds(tile, 1), :].rearrange("p a f -> p (a f)")
                            gate = gates[:, :, :].rearrange("p t e -> p (t e)")[:, bass.ds(tile * EXPERTS + e, 1)]
                            V.scalar_tensor_tensor(out=row, in0=bank_e[i][:, t, :], scalar=gate, in1=row,
                                                   op0=ALU.mult, op1=ALU.add).then_inc(s_e, 1)

        @block.sync
        def _(sp):
            for t, src in ((cond_sb[:, :], condT), (affw_sb[:, :, :], aff_wT), (affb_sb[:, :], aff_b),
                           (modb_sb[:, :], mod_b)):
                sp.dma_start(t, src).then_inc(s_ld_mod, 16)
            sp.dma_start(modw_sb[:, :, :], mod_wT).then_inc(s_ld_modw, 16)
            half = TOKENS // 2
            sp.dma_start(x_all[:, 0:QUAD * P], xT[:, 0:QUAD * P]).then_inc(s_ld_x0, 16)
            sp.dma_start(wk_sb[:, :], wk).then_inc(s_ld_qkv, 16)
            sp.dma_start(wv_sb[:, :], wv).then_inc(s_ld_qkv, 16)
            sp.dma_start(wq_sb[:, :], wq).then_inc(s_ld_qkv, 16)
            sp.dma_start(x_all[:, QUAD * P:half], xT[:, QUAD * P:half]).then_inc(s_ld_x, 16)
            sp.dma_start(x_all[:, half:TOKENS], xT[:, half:TOKENS]).then_inc(s_ld_x, 16)
            sp.dma_start(wpost_sb[:, :, :], wpost.rearrange("(c k) n -> k c n", k=P)).then_inc(s_ld_post, 16)
            sp.dma_start(gate_sb[:, :], gate_wT).then_inc(s_ld_post, 16)
            sp.dma_start(w1_sb[:, :, :], w1.rearrange("e h f -> h e f")).then_inc(s_ld_ffn, 16)
            sp.dma_start(w2_sb[:, :, :], w2.rearrange("e h f -> h e f")).then_inc(s_ld_ffn, 16)
            sp.dma_start(b1_sb[:, :], b1T).then_inc(s_ld_ffn, 16)
            sp.wait_ge(s_zero, 2)
            for i in range(P // EXPERTS):
                sp.dma_start(b2_rows[i * EXPERTS:(i + 1) * EXPERTS, i, :], b2).then_inc(s_ld_ffn, 16)
            sp.wait_ge(s_rt, ROUTE_STEPS["n"])
            before_last = sp.value_load(n_run[0:1, 1:2], min_val=1, max_val=EXPERTS - 1)
            for q in range(QUADS):
                sp.wait_ge(s_e, QUADS + before_last * (QUADS * QUAD) + (q + 1) * QUAD)
                sp.dma_start(out[q * QUAD * P:(q + 1) * QUAD * P, :].rearrange("(t p) c -> p t c", p=P),
                             acc_all[:, q * QUAD:(q + 1) * QUAD, :]).then_inc(s_out, 16)
            sp.wait_ge(s_out, 16 * QUADS)

        @block.tensor
        def _(pe):
            mm = nc.tensor.matmul

            pe.wait_ge(s_ld_mod, 64)
            for m in range(3):
                last = mm(misc[0][:, 0, m * BATCH:(m + 1) * BATCH], affw_sb[:, m, :], cond_sb[:, :],
                          start=(m == 0), stop=True, skip_group_check=True)
            last.then_inc(s_style_mm, 1)
            pe.wait_ge(s_sq, 2)
            for m in range(3):
                last = mm(misc[1][:, 0, m * BATCH:(m + 1) * BATCH], modw_sq[:, m, :], style_sq[:, m, :],
                          start=(m == 0), stop=True, skip_group_check=True)
            last.then_inc(s_power_mm, 1)
            pe.wait_ge(s_power, 1)
            pe.wait_ge(s_const, 3)
            pe.wait_ge(s_ld_qkv, 48)

            def scores(s, j, g):
                need(pe, s_max, 4 * s + g)
                for i in range(2):
                    last = mm(bank_s[:, 2 * i:2 * i + 2, :], q16[:, j, 2 * g + i, :],
                              k16[:, j, g, :, :], start=(i == 0), stop=True, skip_group_check=True)
                last.then_inc(s_s_mm, 1)

            def scores_t(s, j, g):
                need(pe, s_prob, 4 * s + g - 1)
                for par in range(2):
                    mm(bank_t[g % 2][:, par:HPG:2, :], k_pad[:, j, g, par, :],
                       qT[:, j, 2 * g:2 * g + 2, :], start=(par == 0), stop=False, skip_group_check=True)
                for w in range(HPG):
                    last = mm(bank_t[g % 2][:, w, :], pick[:, HPG * g + w, :], neg_max[:, :],
                              start=False, stop=True, skip_group_check=True)
                last.then_inc(s_t_mm, 1)

            def attend(s, j, g):
                pe.wait_ge(s_prob, 4 * s + g + 1)
                need(pe, s_att, 4 * s + g - 1)
                for w in range(HPG):
                    last = mm(att_bank(g)[:, w, :], prob[:, g % 2, w, :], v1[:, j, g, :],
                              start=(w == 0), stop=True, skip_group_check=True)
                last.then_inc(s_av_mm, 1)

            def queries(b, half):
                for c in range(4 * half, 4 * half + 4):
                    last = mm(misc[0][:, c % 4, :], wq_sb[:, c * P:(c + 1) * P], yT[:, :],
                              start=(c % 4 == 0), stop=True, skip_group_check=True)
                last.then_inc(s_q_mm, 1)

            def att_transpose(b, half):
                pe.wait_ge(s_att, 4 * b + 2 * half + 2)
                for c in range(4 * half, 4 * half + 4):
                    last = nc.tensor.transpose(misc[1 + half][:, c % 4, :],
                                               att[:, 2 * c:2 * c + 2, :].rearrange("p h e -> p (h e)"),
                                               ident[:, :])
                last.then_inc(s_attT_mm, 1)

            def slot(s, j):
                a, c, h, d = s + 1, s - 1, s - 2, s - 3
                A, B, C, H, D = has(a), has(s), has(c), has(h), has(d)
                ja = 1 - j
                if C:
                    bank_free(pe, 1, s, "att0")
                    att_transpose(c, 0)
                if B:
                    scores(s, j, 3)
                if C:
                    bank_free(pe, 2, s, "att1")
                    att_transpose(c, 1)
                if A:
                    pe.wait_ge(s_yT, n(a))
                    queries(a, 0)
                if B:
                    bank_free(pe, 1, s, "neg")
                    pe.wait_ge(s_max, 4 * s + 4)
                    nc.tensor.transpose(misc[1][:, 0, :], row_max[:, :], ident[:, :]).then_inc(s_neg_mm, 1)
                if C:
                    if isinstance(s, int) and c == 0:
                        pe.wait_ge(s_ld_post, 32)
                    pe.wait_ge(s_attT, 2 * n(c))
                    for k in range(CHUNKS):
                        last = mm(misc[2][:, 0, :], wpost_sb[:, k, :], attT[:, k, :],
                                  start=(k == 0), stop=(k == CHUNKS - 1))
                    last.then_inc(s_post_mm, 1)
                if B:
                    pe.wait_ge(s_neg, n(s))
                    scores_t(s, j, 0)
                if A:
                    bank_free(pe, 0, s, "q1")
                    queries(a, 1)
                if C:
                    bank_free(pe, 1, s, "kx")
                    pe.wait_ge(s_x1s, n(c))
                    mm(misc[1][:, 0, :], modw_sb[:, 1, :], x1s[:, :], start=True, stop=True).then_inc(s_kx_mm, 1)
                if B:
                    scores_t(s, j, 1)
                if C:
                    pe.wait_ge(s_kxT, n(c))
                    nc.tensor.transpose(misc[1][:, 0, :], kxT[:, :], ident[:, :]).then_inc(s_kxn_mm, 1)
                if D:
                    bank_free(pe, 2, s, "mix")
                    pe.wait_ge(s_mix, n(d))
                    nc.tensor.transpose(misc[2][:, 0, :], mix[:, :], ident[:, :]).then_inc(s_mixT_mm, 1)
                if A:
                    bank_free(pe, 0, s, "kv")
                    for i in range(2):
                        mm(misc[0][:, i, :], wk_sb[:, i * P:(i + 1) * P], yT[:, :],
                           start=(i == 0), stop=True, skip_group_check=True)
                    mm(misc[0][:, 2:4, :].rearrange("p a f -> p (a f)"), yT[:, :], wv_sb[:, :], start=False,
                       stop=True, skip_group_check=True).then_inc(s_kv_mm, 1)
                if B:
                    attend(s, j, 0)
                if C:
                    bank_free(pe, 2, s, "x1n")
                    nc.tensor.transpose(misc[2][:, 0, :], x1T[:, :], ident[:, :]).then_inc(s_x1n_mm, 1)
                if D:
                    bank_free(pe, 1, s, "o")
                    pe.wait_ge(s_mixT, n(d))
                    mm(misc[1][:, 0, :], modw_sb[:, 2, :], mixT[:, :], start=True, stop=True).then_inc(s_o_mm, 1)
                if B:
                    scores_t(s, j, 2)
                if B:
                    attend(s, j, 1)
                if A:
                    pe.wait_ge(s_q16, n(a))
                    pe.wait_ge(s_k16, n(a))
                    scores(a, ja, 0)
                if B:
                    scores_t(s, j, 3)
                if A:
                    scores(a, ja, 1)
                if B:
                    attend(s, j, 2)
                if A:
                    scores(a, ja, 2)
                if has(a + 1):
                    bank_free(pe, 0, s, "y")
                    pe.wait_ge(s_xs, n(a + 1))
                    mm(misc[0][:, 0, :], modw_sb[:, 0, :], xs[:, j, :], start=True, stop=True).then_inc(s_y_mm, 1)
                if B:
                    attend(s, j, 3)
                if D:
                    bank_free(pe, 2, s, "log")
                    pe.wait_ge(s_tok, n(d))
                    mm(misc[2][:, 0, 0:EXPERTS], tokT[:, :], gate_sb[:, :], start=True, stop=True).then_inc(s_log_mm, 1)

            slots(pe, slot)

            pe.wait_ge(s_log, BATCH)
            pe.wait_ge(s_rt, ROUTE_STEPS["count"])
            mm(misc[0][:, 0, 0:EXPERTS], ones[:, :], count[:, :], start=True, stop=True).then_inc(s_cnt_mm, 1)
            pe.wait_ge(s_rt, ROUTE_STEPS["gates"])
            for i in range(2):
                src = gates[:, i * 16:(i + 1) * 16, :].rearrange("p t e -> p (t e)")
                last = nc.tensor.transpose(misc[1][:, i, :], src, ident[:, :])
            last.then_inc(s_gT_mm, 1)
            pe.wait_ge(s_gT, 1)
            pe.wait_ge(s_ld_ffn, 16 * (3 + P // EXPERTS))
            for q in range(QUADS):
                need(pe, s_e, q - 1)
                for t in range(QUAD):
                    i = q * QUAD + t
                    last = mm(bank_e[q % 2][:, t, :], gatesT[:, i // 16, :], b2_rows[:, i % 16, :],
                              start=(t == 0), stop=True, skip_group_check=True)
                last.then_inc(s_b2_mm, 1)
            pe.wait_ge(s_e, QUADS)
            pe.wait_ge(s_tok_kept, BATCH)
            pe.wait_ge(s_rt, ROUTE_STEPS["n"])
            runs = pe.value_load(n_run[0:1, 0:1], min_val=2, max_val=EXPERTS)

            with pe.Fori(0, runs) as k:
                e = pe.value_load(order[0:1, bass.ds(k, 1)], min_val=0, max_val=EXPERTS - 1)
                with pe.Fori(0, QUADS // 2) as two:
                    q = two * 2
                    for i in range(2):
                        pe.wait_ge(s_w1, k + 1)
                        mm(bank_t[i][:, :, :], w1_now[:, :], tok_all[:, bass.ds((q + i) * QUAD * P, QUAD * P)],
                           start=True, stop=True).then_inc(s_h_mm, 1)
                    for i in range(2):
                        pe.wait_ge(s_h, k * QUADS + q + i + 1)
                        pe.wait_ge(s_e, QUADS + (k * QUADS + q + i - 1) * QUAD)
                        for t in range(QUAD):
                            last = mm(bank_e[i][:, t, :], hT[:, i, t * P:(t + 1) * P],
                                      w2_sb[:, bass.ds(e, 1), :].rearrange("p a f -> p (a f)"),
                                      start=(t == 0), stop=True, skip_group_check=True)
                        last.then_inc(s_e_mm, 1)

        @block.scalar
        def _(act):
            def f(out_, in_, func=ACT.Copy, **kw):
                return nc.scalar.activation(out_, in_, func, **kw)

            act.wait_ge(s_ld_mod, 64)
            act.wait_ge(s_style_mm, 1)
            gains = (1.0 / COND ** 0.5, 1.0, 1.0)
            for m in range(3):
                f(style[:, m, :], misc[0][:, 0, m * BATCH:(m + 1) * BATCH], ACT.Identity,
                  bias=affb_sb[:, m:m + 1], scale=gains[m]).then_inc(s_style, 1)
            act.wait_ge(s_power, 1)
            f(root[:, :, :], power[:, :, :], ACT.Sqrt).then_inc(s_root, 1)
            act.wait_ge(s_demod, 5)
            act.wait_ge(s_zero, 5)

            def exp_scores(s, g):
                act.wait_ge(s_t_mm, 4 * s + g + 1)
                need(act, s_av_mm, 4 * s + g - 1)
                f(prob[:, g % 2, :, :], bank_t[g % 2][:, :, :], ACT.Exp, scale=KEY_SCALE).then_inc(s_prob, 1)

            def copy_q(b, j, half):
                act.wait_ge(s_q_mm, 2 * b + half + 1)
                need(act, s_t_mm, 4 * n(b - 2))
                need(act, s_q16, n(b - 2))
                f(qT[:, j, 4 * half:4 * half + 4, :], misc[0][:, :, :]).then_inc(s_q, 1)

            def copy_att(b, half):
                need(act, s_post_mm, n(b - 1))
                act.wait_ge(s_attT_mm, 2 * b + half + 1)
                f(attT[:, 4 * half:4 * half + 4, :], misc[1 + half][:, :, :]).then_inc(s_attT, 1)

            def slot(s, j):
                a, c, h, d = s + 1, s - 1, s - 2, s - 3
                A, B, C, H, D = has(a), has(s), has(c), has(h), has(d)
                ja, jc, jh, jd = 1 - j, 1 - j, j, 1 - j
                if C:
                    copy_att(c, 0)
                    copy_att(c, 1)
                if A:
                    copy_q(a, ja, 0)
                if B:
                    act.wait_ge(s_neg_mm, n(s))
                    need(act, s_t_mm, 4 * n(s - 1))
                    f(neg_max[:, :], misc[1][:, 0, :], scale=-1.0).then_inc(s_neg, 1)
                if C:
                    act.wait_ge(s_x1T, n(c))
                    need(act, s_kx_mm, n(c - 1))
                    act.wait_ge(s_demod, 5)
                    f(x1s[:, :], x1T[:, :], scale=style[:, 1, bass.ds(c, 1)]).then_inc(s_x1s, 1)
                if B:
                    exp_scores(s, 0)
                if A:
                    copy_q(a, ja, 1)
                if C:
                    act.wait_ge(s_kx_mm, n(c))
                    need(act, s_kxn_mm, n(c - 1))
                    act.wait_ge(s_demod, 5)
                    f(kxT[:, :], misc[1][:, 0, :], ACT.Identity, scale=demod[:, 1, bass.ds(c, 1)],
                      bias=modb_sb[:, 1:2]).then_inc(s_kxT, 1)
                if B:
                    exp_scores(s, 1)
                if C:
                    act.wait_ge(s_kxn_mm, n(c))
                    need(act, s_lo, 4 * n(c - 2))
                    need(act, s_hi, 4 * n(c - 2))
                    f(kx2[:, jc, :].rearrange("p (r f) -> p r f", r=2),
                      misc[1][:, 0:1, :].to_broadcast([P, 2, P])).then_inc(s_kx2, 1)
                if D:
                    act.wait_ge(s_mixT_mm, n(d))
                    need(act, s_o_mm, n(d - 1))
                    act.wait_ge(s_style, 3)
                    f(mixT[:, :], misc[2][:, 0, :], scale=style[:, 2, bass.ds(d, 1)]).then_inc(s_mixT, 1)
                if A:
                    act.wait_ge(s_kv_mm, n(a))
                    need(act, s_t_mm, 4 * n(a - 2))
                    need(act, s_k16, n(a - 2))
                    for src in range(2):
                        for par in range(2):
                            f(k_pad[par * KEY:(par + 1) * KEY, ja, src:GROUPS:2, par, :],
                              misc[0][src * KEY:(src + 1) * KEY, 0:2, :]).then_inc(s_k, 1)
                if A:
                    act.wait_ge(s_q, 2 * n(a))
                    need(act, s_s_mm, 4 * n(a - 2))
                    f(q16[:, ja, :, :], qT[:, ja, :, :]).then_inc(s_q16, 1)
                if H:
                    act.wait_ge(s_shifted, n(h))
                    need(act, s_mix, n(h - 2))
                    need(act, s_hi, 4 * n(h - 2))
                    f(weight[:, jh, :, :], shifted[:, :, :], ACT.Exp, scale=MIX_SCALE).then_inc(s_weight, 1)
                if A:
                    need(act, s_av_mm, 4 * n(a - 2))
                    f(v1[:, ja, :, 0:KEY],
                      misc[0][:, 2:4, :].rearrange("p a (g e) -> p (a g) e", e=KEY)).then_inc(s_v, 1)
                if B:
                    exp_scores(s, 2)
                if C:
                    act.wait_ge(s_x1n_mm, n(c))
                    act.wait_ge(s_zero, 5)
                    f(acc_all[:, bass.ds(c, 1), :].rearrange("p a f -> p (a f)"),
                      misc[2][:, 0, :]).then_inc(s_x1n, 1)
                if D:
                    act.wait_ge(s_o_mm, n(d))
                    need(act, s_log_mm, n(d - 1))
                    need(act, s_tok_kept, n(d - 1))
                    act.wait_ge(s_demod, 5)
                    f(tokT[:, :], misc[1][:, 0, :], ACT.Identity, scale=demod[:, 2, bass.ds(d, 1)],
                      bias=modb_sb[:, 2:3]).then_inc(s_tok, 1)
                if B:
                    exp_scores(s, 3)
                if has(a + 1):
                    act.wait_ge(s_y_mm, n(a + 1))
                    need(act, s_yT, n(a))
                    act.wait_ge(s_demod, 5)
                    f(y_raw[:, :], misc[0][:, 0, :], ACT.Identity, scale=demod[:, 0, bass.ds(a + 1, 1)],
                      bias=modb_sb[:, 0:1]).then_inc(s_y_raw, 1)
                if D:
                    act.wait_ge(s_log_mm, n(d))
                    act.wait_ge(s_ld_mod, 64)
                    f(logits[:, bass.ds(d, 1), :].rearrange("p a e -> p (a e)"),
                      misc[2][:, 0, 0:EXPERTS]).then_inc(s_log, 1)

            slots(act, slot)

            act.wait_ge(s_rt, ROUTE_STEPS["exp"])
            f(gates[:, :, :], rest[:, :, :], ACT.Exp).then_inc(s_rt_exp, 1)
            act.wait_ge(s_gT_mm, 1)
            f(gatesT[:, :, :], misc[1][:, 0:2, :]).then_inc(s_gT, 1)
            act.wait_ge(s_ld_ffn, 16 * (3 + P // EXPERTS))
            act.wait_ge(s_rt, ROUTE_STEPS["n"])
            runs = act.value_load(n_run[0:1, 0:1], min_val=2, max_val=EXPERTS)
            with act.Fori(0, runs) as k:
                with act.Fori(0, QUADS // 2) as two:
                    q = two * 2
                    for i in range(2):
                        act.wait_ge(s_h_mm, k * QUADS + q + i + 1)
                        f(hT[:, i, :], bank_t[i][:, :, :].rearrange("p t f -> p (t f)"), ACT.Relu,
                          bias=b1_now[:, :]).then_inc(s_h, 1)

        @block.gpsimd
        def _(pool):
            G = nc.gpsimd
            G.memset(ident[:, :], 0.0).then_inc(s_blank, 1)
            G.memset(pick[:, :, :], 0.0).then_inc(s_blank, 1)
            G.memset(before[:, :, :], 0.0).then_inc(s_const, 1)
            pool.wait_ge(s_blank, 2)
            pool.wait_ge(s_const, 1)
            G.affine_select(out=ident[:, :], in_=ident[:, :], compare_op=ALU.not_equal, fill=1.0, base=0,
                            pattern=[[-1, P]], channel_multiplier=1).then_inc(s_const, 1)
            G.affine_select(out=pick[:, :, :], in_=pick[:, :, :], compare_op=ALU.not_equal, fill=1.0, base=0,
                            pattern=[[-1, HEADS], [0, P]], channel_multiplier=1).then_inc(s_const, 1)

            pool.wait_ge(s_style, 3)

            def slot(s, j):
                a, c, h, d = s + 1, s - 1, s - 2, s - 3
                A, B, C, H, D = has(a), has(s), has(c), has(h), has(d)
                ja, jc, jh, jd = 1 - j, 1 - j, j, 1 - j

                def xs_of(b, jb):
                    need(pool, s_y_mm, n(b - 2))
                    pool.wait_ge(s_style, 3)
                    G.tensor_tensor(xs[:, jb, :], x_all[:, col(b)],
                                    style[:, 0, bass.ds(b, 1)].to_broadcast([P, P]), ALU.mult).then_inc(s_xs, 1)

                if D:
                    pool.wait_ge(s_weight, n(d))
                    need(pool, s_msum, n(d - 1))
                    G.tensor_tensor(mix_hi[:, :, :].rearrange("p r (h e) -> p r h e", e=MD),
                                    weight[:, jd, MH // 2:MH, :].unsqueeze(3).to_broadcast([P, MH // 2, MH, MD]),
                                    bass.AP(kx2, jd * 2 * P + MD * MH // 2,
                                            [[4 * P, P], [MD, MH // 2], [MD, MH], [1, MD]]),
                                    ALU.mult).then_inc(s_hi, 1)
                    for i, r in enumerate((4, 2, 1)):
                        pool.wait_ge(s_hi, 4 * d + i + 1)
                        G.tensor_tensor(mix_hi[:, 0:r, :], mix_hi[:, 0:r, :], mix_hi[:, r:2 * r, :],
                                        ALU.add).then_inc(s_hi, 1)
                if C:
                    pool.wait_ge(s_kx2, n(c))
                    need(pool, s_score, n(c - 1))
                    G.tensor_tensor(pair[:, :, :],
                                    bass.AP(kx2, jc * 2 * P, [[4 * P, P], [0, SHIFTS], [1, P]]),
                                    bass.AP(kx2, jc * 2 * P, [[4 * P, P], [MD, SHIFTS], [1, P]]),
                                    ALU.mult).then_inc(s_pair, 1)
                if isinstance(s, int) and s == -2:
                    pool.wait_ge(s_ld_x0, 16)
                if isinstance(s, int) and s + 2 == QUAD:
                    pool.wait_ge(s_ld_x, 32)
                if has(s + 2):
                    xs_of(s + 2, j)
                if D:
                    pool.wait_ge(s_tok, n(d))
                    pool.wait_ge(s_ld_x0, 16)
                    G.tensor_copy(tok_all[:, col(d)], tokT[:, :]).then_inc(s_tok_kept, 1)
                if isinstance(s, int) and s == 0:
                    for e in range(EXPERTS):
                        G.memset(index8[:, e:e + 1], float(e))
                        last = G.memset(rank8[:, e:e + 1], float(EXPERTS - e))
                        if e:
                            last = G.memset(before[:, e, 0:e], 1.0)
                    last.then_inc(s_const, 1)

            slots(pool, slot)


_INS = ("xT", "condT", "aff_wT", "aff_b", "mod_wT", "mod_b", "wq", "wk", "wv", "wpost", "gate_wT",
        "w1", "b1T", "w2", "b2")


def kernel(x, cond_512, L0_cond_weight, L0_cond_bias, L0_cond_affine_w, L0_cond_affine_b, L0_attn_Wq,
           L0_attn_Wk, L0_attn_Wv, L0_attn_Wpost, L0_cond2_k_aff_w, L0_cond2_k_aff_b, L0_cond2_k_w,
           L0_cond2_k_b, L0_cond2_o_aff_w, L0_cond2_o_aff_b, L0_cond2_o_w, L0_cond2_o_b, L0_ffn_gate_w,
           L0_ffn_W1, L0_ffn_b1, L0_ffn_W2, L0_ffn_b2):
    import concourse.bacc as bacc
    from concourse.bass_utils import run_bass_kernel_spmd

    arrays = {
        "xT": np.asarray(x).reshape(TOKENS, P).T,
        "condT": np.asarray(cond_512).T,
        "aff_wT": np.stack([np.asarray(w).T for w in (L0_cond_affine_w, L0_cond2_k_aff_w, L0_cond2_o_aff_w)], 1),
        "aff_b": np.stack([np.asarray(w) for w in (L0_cond_affine_b, L0_cond2_k_aff_b, L0_cond2_o_aff_b)], 1),
        "mod_wT": np.stack([np.asarray(w).T for w in (L0_cond_weight, L0_cond2_k_w, L0_cond2_o_w)], 1),
        "mod_b": np.stack([np.asarray(w) for w in (L0_cond_bias, L0_cond2_k_b, L0_cond2_o_b)], 1),
        "wq": L0_attn_Wq, "wk": L0_attn_Wk, "wv": L0_attn_Wv, "wpost": L0_attn_Wpost,
        "gate_wT": np.asarray(L0_ffn_gate_w).T,
        "w1": L0_ffn_W1, "b1T": np.asarray(L0_ffn_b1).T, "w2": L0_ffn_W2, "b2": L0_ffn_b2,
    }
    arrays = {k: np.ascontiguousarray(v) for k, v in arrays.items()}
    nc = bacc.Bacc("TRN2", target_bir_lowering=False, num_devices=1)
    ins = [nc.dram_tensor(f"in_{k}", arrays[k].shape, mybir.dt.from_np(arrays[k].dtype),
                          kind="ExternalInput").ap() for k in _INS]
    out = nc.dram_tensor("out", (TOKENS, P), F32, kind="ExternalOutput").ap()
    build(nc, *ins, out)
    result = run_bass_kernel_spmd(nc, [{f"in_{k}": arrays[k] for k in _INS}], core_ids=[0])
    return result.results[0]["out"].reshape(BATCH, P, P)
```

```python
from contextlib import ExitStack

import numpy as np

import concourse.bass as bass
from concourse import mybir

F32 = mybir.dt.float32
BF16 = mybir.dt.bfloat16
I32 = mybir.dt.int32
ALU = mybir.AluOpType
ACT = mybir.ActivationFunctionType
AX = mybir.AxisListType

P = 128
BATCH = 32
TOKENS = BATCH * P
COND = 64
GROUPS, HPG, KEY = 4, 4, 64
HEADS = GROUPS * HPG
CHUNKS = HEADS * KEY // P
MH, MD = 16, 8
SHIFTS = MH // 2 + 1
EXPERTS = 8
CAP = int(1.25 * TOKENS / EXPERTS)
QUAD = 4
QUADS = BATCH // QUAD
CLAMP = 256.0
EPS = 1e-8
KEY_SCALE = 1.0 / KEY ** 0.5
MIX_SCALE = 1.0 / MD ** 0.5
EARLY, RECENT = range(BATCH - QUAD), range(BATCH - QUAD, BATCH)
LOOP_FROM, LOOP_TO = 4, BATCH - 2


def build(nc, xT, condT, aff_wT, aff_b, mod_wT, mod_b, wq, wk, wv, wpost, gate_wT,
          w1, b1T, w2, b2, out):
    ctx = ExitStack()
    with ctx:
        def sb(name, shape, dt=F32):
            return ctx.enter_context(nc.sbuf_tensor(name, shape, dt))

        def pb(name, shape, dt=F32):
            return ctx.enter_context(nc.psum_tensor(name, shape, dt))

        def sem(name):
            return ctx.enter_context(nc.semaphore(name))

        x_all = sb("x_all", [P, TOKENS])
        tok_all = sb("tok_all", [P, TOKENS])
        acc_all = sb("acc_all", [P, BATCH, P])
        logits = sb("logits", [P, BATCH, EXPERTS])
        ident = sb("ident", [P, P])
        ones = sb("ones", [P, P])
        own_head = sb("own_head", [P, HEADS])
        cond_sb = sb("cond_sb", [COND, BATCH])
        affw_sb = sb("affw_sb", [COND, 3, P])
        affb_sb = sb("affb_sb", [P, 3])
        modw_sb = sb("modw_sb", [P, 3, P])
        modb_sb = sb("modb_sb", [P, 3])
        wq_sb = sb("wq_sb", [P, HEADS * KEY])
        wk_sb = sb("wk_sb", [P, GROUPS * KEY])
        wv_sb = sb("wv_sb", [P, GROUPS * KEY])
        wpost_sb = sb("wpost_sb", [P, CHUNKS, P])
        gate_sb = sb("gate_sb", [P, EXPERTS])
        w1_sb = sb("w1_sb", [P, EXPERTS, P])
        w2_sb = sb("w2_sb", [P, EXPERTS, P])
        b1_sb = sb("b1_sb", [P, EXPERTS])
        b2_rows = sb("b2_rows", [P, P // EXPERTS, P])
        style = sb("style", [P, 3, BATCH])
        demod = sb("demod", [P, 3, BATCH])
        style_sq = sb("style_sq", [P, 3, BATCH])
        modw_sq = sb("modw_sq", [P, 3, P])
        power = sb("power", [P, 3, BATCH])
        root = sb("root", [P, 3, BATCH])
        inv_root = sb("inv_root", [P, 3, BATCH])
        newton = sb("newton", [P, 3, BATCH])
        xs = sb("xs", [P, 2, P])
        y_raw = sb("y_raw", [P, P])
        yT = sb("yT", [P, P])
        qT = sb("qT", [P, 2, HEADS, P])
        q16 = sb("q16", [P, 2, HEADS, P], BF16)
        k_one = sb("k_one", [P, 2, GROUPS, P])
        k16 = sb("k16", [P, 2, GROUPS, P], BF16)
        v1 = sb("v1", [P, 2, GROUPS, KEY + 1])
        row_max = sb("row_max", [P, P])
        neg_max = sb("neg_max", [P, P])
        prob = sb("prob", [P, 2, HPG, P])
        recip_den = sb("recip_den", [P, 2, HPG])
        att = sb("att", [P, HEADS, KEY])
        attT = sb("attT", [P, CHUNKS, P])
        x1s = sb("x1s", [P, P])
        kxT = sb("kxT", [P, P])
        kx2 = sb("kx2", [P, 2, 2 * P])
        pair = sb("pair", [P, SHIFTS, P])
        score = sb("score", [P, MH, 2 * MH])
        h_max = sb("h_max", [P, MH])
        shifted = sb("shifted", [P, MH, MH])
        weight = sb("weight", [P, 2, MH, MH])
        h_den = sb("h_den", [P, MH])
        h_rden = sb("h_rden", [P, MH])
        mix_lo = sb("mix_lo", [P, MH // 2, P])
        mix_hi = sb("mix_hi", [P, MH // 2, P])
        mix_sum = sb("mix_sum", [P, P])
        mix = sb("mix", [P, P])
        mixT = sb("mixT", [P, P])
        r_max = sb("r_max", [P, BATCH])
        r_key = sb("r_key", [P, BATCH])
        gates = sb("gates", [P, BATCH, EXPERTS])
        rest = sb("rest", [P, BATCH, EXPERTS])
        cand = sb("cand", [P, BATCH, EXPERTS])
        first = sb("first", [P, BATCH, EXPERTS])
        chosen = sb("chosen", [P, BATCH, EXPERTS])
        rank8 = sb("rank8", [P, EXPERTS])
        index8 = sb("index8", [P, EXPERTS])
        count = sb("count", [P, EXPERTS])
        keep = sb("keep", [P, EXPERTS])
        t88 = sb("t88", [P, EXPERTS, EXPERTS])
        key = sb("key", [P, EXPERTS])
        place = sb("place", [P, EXPERTS])
        kept = sb("kept", [P, 1])
        order_f = sb("order_f", [P, EXPERTS])
        order = sb("order", [P, EXPERTS], I32)
        n_run = sb("n_run", [P, 2], I32)
        gatesT = sb("gatesT", [P, 2, P])
        w1_now = sb("w1_now", [P, P])
        b1_now = sb("b1_now", [P, 1])
        hT = sb("hT", [P, 2, QUAD * P])
        w2_run = sb("w2_run", [P, EXPERTS, P])
        gate_run = sb("gate_run", [P, EXPERTS, BATCH])

        bank_s = pb("bank_s", [P, HPG, P])
        bank_t = [pb(f"bank_t{i}", [P, HPG, P]) for i in range(2)]
        bank_a = [pb(f"bank_a{i}", [P, 512]) for i in range(2)]
        misc = [pb(f"misc{i}", [P, QUAD, P]) for i in range(3)]
        bank_x = [b[:, :, :] for b in bank_t] + [b[:, :].rearrange("p (t f) -> p t f", f=P) for b in bank_a]
        bank_e = [bank_s, misc[2]]
        bank_b = bank_x[2:] + [misc[0][:, :, :], misc[1][:, :, :]]

        def att_bank(g):
            return bank_a[g % 2][:, 0:HPG * (KEY + 1)].rearrange("p (w e) -> p w e", e=KEY + 1)

        s_ld_mod, s_ld_modw, s_ld_x0, s_ld_x, s_ld_qkv = (sem("ld_mod"), sem("ld_modw"), sem("ld_x0"),
                                                         sem("ld_x"), sem("ld_qkv"))
        s_ld_post, s_ld_ffn = sem("ld_post"), sem("ld_ffn")
        s_out = sem("out_written")
        s_const, s_blank, s_zero, s_warm = sem("const"), sem("blank"), sem("zero"), sem("warm")
        s_style_mm, s_style, s_sq, s_power_mm = sem("style_mm"), sem("style"), sem("sq"), sem("power_mm")
        s_power, s_root, s_demod = sem("power"), sem("root"), sem("demod")
        s_xs, s_y_mm, s_y_raw, s_yT, s_xy = sem("xs"), sem("y_mm"), sem("y_raw"), sem("yT"), sem("xy")
        s_q_mm, s_q, s_kv_mm, s_k, s_v = sem("q_mm"), sem("q"), sem("kv_mm"), sem("k"), sem("v")
        s_q16, s_k16 = sem("q16"), sem("k16")
        s_s_mm, s_max, s_t_mm, s_prob = sem("s_mm"), sem("max"), sem("t_mm"), sem("prob")
        s_av_mm, s_rden, s_att = sem("av_mm"), sem("rden"), sem("att")
        s_neg_mm, s_neg = sem("neg_mm"), sem("neg")
        s_own = sem("own")
        s_attT_mm, s_attT = sem("attT_mm"), sem("attT")
        s_post_mm, s_x1T, s_x1s, s_kx_mm, s_kxT = sem("post_mm"), sem("x1T"), sem("x1s"), sem("kx_mm"), sem("kxT")
        s_kxn_mm, s_kx2, s_x1n_mm, s_x1n = sem("kxn_mm"), sem("kx2"), sem("x1n_mm"), sem("x1n")
        s_pair, s_score, s_twice, s_mirror = sem("pair"), sem("score"), sem("twice"), sem("mirror")
        s_hmax, s_shifted, s_weight = sem("hmax"), sem("shifted"), sem("weight")
        s_hden, s_hrden, s_lo, s_hi = sem("hden"), sem("hrden"), sem("lo"), sem("hi")
        s_msum, s_mix, s_mixT_mm, s_mixT = sem("msum"), sem("mix"), sem("mixT_mm"), sem("mixT")
        s_o_mm, s_tok, s_log_mm, s_log = sem("o_mm"), sem("tok"), sem("log_mm"), sem("log")
        s_rt, s_rt_exp, s_cnt_mm, s_gT_mm, s_gT = sem("rt"), sem("rt_exp"), sem("cnt_mm"), sem("gT_mm"), sem("gT")
        s_b2_mm, s_b2 = sem("b2_mm"), sem("b2")
        s_gate_now, s_w2_now, s_b1 = sem("gate_now"), sem("w2_now"), sem("b1")
        s_w1, s_h_mm, s_h, s_e_mm = sem("w1"), sem("h_mm"), sem("h"), sem("e_mm")
        s_e = sem("e")

        ROUTE_STEPS = {}

        def n(b):
            return b + 1

        def need(eng, s, v):
            if not (isinstance(v, int) and v <= 0):
                eng.wait_ge(s, v)

        def has(b):
            return not isinstance(b, int) or 0 <= b < BATCH

        def bank_users(bank, s):
            a, c, h, d = s + 1, s - 1, s - 2, s - 3
            return ((("q0", a, [(s_q, 4 * a + 2)]), ("q1", a, [(s_q, 4 * a + 4)]),
                     ("kv", a, [(s_v, n(a)), (s_k, 2 * n(a))]), ("y", a + 1, [(s_y_raw, n(a + 1))])),
                    (("att0", c, [(s_attT, 2 * c + 1)]), ("neg", s, [(s_neg, n(s))]), ("kx", c, [(s_kxT, n(c))]),
                     ("kxn", c, [(s_kx2, n(c))]), ("o", d, [(s_tok, n(d))])),
                    (("att1", c, [(s_attT, 2 * c + 2)]), ("post", c, [(s_x1T, n(c))]), ("mix", d, [(s_mixT, n(d))])))[bank]

        def bank_free(eng, bank, s, use):
            now = bank_users(bank, s)
            at = [u[0] for u in now].index(use)
            for _, b, readers in (*reversed(now[:at]), *reversed(bank_users(bank, s - 1))):
                if has(b):
                    for sm, v in readers:
                        eng.wait_ge(sm, v)
                    return

        def slots(eng, slot):
            for s in range(-2, LOOP_FROM):
                slot(s, s % 2)
            with eng.Fori(LOOP_FROM // 2, LOOP_TO // 2) as two:
                slot(two * 2, 0)
                slot(two * 2 + 1, 1)
            for s in range(LOOP_TO, BATCH + 3):
                slot(s, s % 2)

        def s_is(s, number):
            return isinstance(s, int) and s == number

        def late(s):
            return isinstance(s, int) and s > BATCH

        def col(b):
            return bass.ds(b * P, P)

        def qkv_bank(b, use):
            return misc[("q0", "q1", "kv").index(use)] if s_is(b, 0) else misc[0]

        block = ctx.enter_context(nc.Block())

        @block.vector
        def _(dve):
            V = nc.vector
            V.memset(ones[:, :], 1.0).then_inc(s_zero, 1)
            V.memset(b2_rows[:, :, :], 0.0).then_inc(s_zero, 1)
            V.memset(k_one[KEY:P, :, :, :], 0.0).then_inc(s_zero, 1)
            V.memset(k16[KEY:P, :, :, :], 0.0).then_inc(s_zero, 1)
            dve.wait_ge(s_zero, 3)
            V.memset(k_one[KEY:KEY + HEADS, :, :, :], 1.0).then_inc(s_zero, 1)
            V.memset(v1[:, :, :, :], 1.0).then_inc(s_zero, 1)
            V.memset(row_max[:, :], 0.0).then_inc(s_zero, 1)

            dve.wait_ge(s_ld_modw, 16)
            V.tensor_tensor(modw_sq[:, :, :], modw_sb[:, :, :], modw_sb[:, :, :], ALU.mult).then_inc(s_sq, 1)
            dve.wait_ge(s_style, 3)
            V.tensor_tensor(style_sq[:, :, :], style[:, :, :], style[:, :, :], ALU.mult).then_inc(s_sq, 1)
            dve.wait_ge(s_power_mm, 1)
            V.tensor_scalar(power[:, :, :], misc[1][:, 0, 0:3 * BATCH].rearrange("p (m b) -> p m b", m=3),
                            EPS, None, ALU.add).then_inc(s_power, 1)
            dve.wait_ge(s_root, 1)
            V.reciprocal(inv_root[:, :, :], root[:, :, :]).then_inc(s_demod, 1)
            dve.wait_ge(s_demod, 1)
            V.tensor_tensor(newton[:, :, :], inv_root[:, :, :], inv_root[:, :, :], ALU.mult).then_inc(s_demod, 1)
            dve.wait_ge(s_demod, 2)
            V.tensor_tensor(newton[:, :, :], newton[:, :, :], power[:, :, :], ALU.mult).then_inc(s_demod, 1)
            dve.wait_ge(s_demod, 3)
            V.tensor_scalar(newton[:, :, :], newton[:, :, :], -0.5, 1.5, ALU.mult, ALU.add).then_inc(s_demod, 1)
            dve.wait_ge(s_demod, 4)
            V.tensor_tensor(demod[:, :, :], newton[:, :, :], inv_root[:, :, :], ALU.mult).then_inc(s_demod, 1)
            dve.wait_ge(s_zero, 7)

            def group_max(s, g):
                dve.wait_ge(s_s_mm, 4 * s + g + 1)
                need(dve, s_neg_mm, n(s - 1))
                V.tensor_reduce(row_max[:, KEY + HPG * g:KEY + HPG * (g + 1)], bank_s[:, :, :], AX.X,
                                ALU.max).then_inc(s_max, 1)

            def invert(s, g):
                dve.wait_ge(s_av_mm, 4 * s + g + 1)
                need(dve, s_att, 4 * s + g - 1)
                V.reciprocal(recip_den[:, g % 2, :].unsqueeze(2), att_bank(g)[:, :, KEY:KEY + 1]).then_inc(s_rden, 1)

            def normalise(s, g):
                need(dve, s_attT_mm, 2 * n(s - 1))
                dve.wait_ge(s_rden, 4 * s + g + 1)
                V.tensor_tensor(att[:, HPG * g:HPG * (g + 1), :], att_bank(g)[:, :, 0:KEY],
                                recip_den[:, g % 2, :].unsqueeze(2).to_broadcast([P, HPG, KEY]),
                                ALU.mult).then_inc(s_att, 1)

            steps = [0]

            def step(ins):
                steps[0] += 1
                ins.then_inc(s_rt, 1)
                dve.wait_ge(s_rt, steps[0])
                return steps[0]

            def over_e(t):
                return t.unsqueeze(2).to_broadcast([P, t.shape[1], EXPERTS])

            def over_t(t, tiles=range(BATCH)):
                return t[:, :].unsqueeze(1).to_broadcast([P, len(tiles), EXPERTS])

            def part(t, tiles):
                return t[:, tiles[0]:tiles[-1] + 1]

            def first_choice(tiles):
                lg, rs, cd, fi = (part(t, tiles) for t in (logits, rest, cand, first))
                top, key_ = part(r_max, tiles), part(r_key, tiles)
                step(V.tensor_reduce(top, lg, AX.X, ALU.max))
                ROUTE_STEPS["exp", tiles[0]] = step(V.tensor_tensor(rs, lg, over_e(top), ALU.subtract))
                step(V.scalar_tensor_tensor(out=cd, in0=rs, scalar=0.0, in1=over_t(rank8, tiles),
                                            op0=ALU.is_equal, op1=ALU.mult))
                step(V.tensor_reduce(key_, cd, AX.X, ALU.max))
                step(V.tensor_tensor(fi, over_t(rank8, tiles), over_e(key_), ALU.is_equal))

            def second_choice(tiles, exps):
                rs, cd, fi, ch, gt = (part(t, tiles) for t in (rest, cand, first, chosen, gates))
                top, key_ = part(r_max, tiles), part(r_key, tiles)
                dve.wait_ge(s_rt_exp, exps)
                step(V.scalar_tensor_tensor(out=rs, in0=fi, scalar=-2.0, in1=gt, op0=ALU.mult, op1=ALU.add))
                step(V.tensor_reduce(top, rs, AX.X, ALU.max))
                step(V.tensor_tensor(cd, rs, over_e(top), ALU.is_equal))
                step(V.tensor_tensor(cd, cd, over_t(rank8, tiles), ALU.mult))
                step(V.tensor_reduce(key_, cd, AX.X, ALU.max))
                step(V.tensor_tensor(ch, over_t(rank8, tiles), over_e(key_), ALU.is_equal))
                step(V.tensor_tensor(ch, ch, fi, ALU.add))

            def slot(s, j):
                a, c, h, d = s + 1, s - 1, s - 2, s - 3
                A, B, C, H, D = has(a), has(s), has(c), has(h), has(d)
                ja, jc, jh, jd = 1 - j, 1 - j, j, 1 - j
                if B:
                    group_max(s, 3)
                if A:
                    dve.wait_ge(s_yT, n(a))
                    V.tensor_tensor(x_all[:, col(a)], x_all[:, col(a)], yT[:, :], ALU.add).then_inc(s_xy, 1)
                if D:
                    dve.wait_ge(s_weight, n(d))
                    need(dve, s_mix, n(d - 1))
                    V.tensor_tensor(mix_lo[:, :, :].rearrange("p r (h e) -> p r h e", e=MD),
                                    weight[:, jd, 0:MH // 2, :].unsqueeze(3).to_broadcast([P, MH // 2, MH, MD]),
                                    bass.AP(kx2, jd * 2 * P, [[4 * P, P], [MD, MH // 2], [MD, MH], [1, MD]]),
                                    ALU.mult).then_inc(s_lo, 1)
                if D:
                    V.tensor_reduce(h_den[:, :], weight[:, jd, :, :].rearrange("p r h -> p h r"), AX.X,
                                    ALU.add).then_inc(s_hden, 1)
                    dve.wait_ge(s_lo, 4 * d + 1)
                    V.tensor_tensor(mix_lo[:, 0:4, :], mix_lo[:, 0:4, :], mix_lo[:, 4:8, :], ALU.add).then_inc(s_lo, 1)
                if C:
                    dve.wait_ge(s_post_mm, n(c))
                    dve.wait_ge(s_xy, n(c))
                    V.tensor_tensor(x_all[:, col(c)], misc[2][:, 0, :], x_all[:, col(c)], ALU.add).then_inc(s_x1T, 1)
                if D:
                    dve.wait_ge(s_hden, n(d))
                    V.reciprocal(h_rden[:, :], h_den[:, :]).then_inc(s_hrden, 1)
                    dve.wait_ge(s_lo, 4 * d + 2)
                    V.tensor_tensor(mix_lo[:, 0:2, :], mix_lo[:, 0:2, :], mix_lo[:, 2:4, :], ALU.add).then_inc(s_lo, 1)
                    dve.wait_ge(s_lo, 4 * d + 3)
                    V.tensor_tensor(mix_lo[:, 0, :], mix_lo[:, 0, :], mix_lo[:, 1, :], ALU.add).then_inc(s_lo, 1)
                def mixed():
                    if D:
                        dve.wait_ge(s_lo, 4 * d + 4)
                        dve.wait_ge(s_hi, 4 * d + 4)
                        V.tensor_tensor(mix_sum[:, :], mix_lo[:, 0, :], mix_hi[:, 0, :], ALU.add).then_inc(s_msum, 1)
                        dve.wait_ge(s_hrden, n(d))
                        dve.wait_ge(s_msum, n(d))
                        need(dve, s_mixT_mm, n(d - 1))
                        V.tensor_tensor(mix[:, :].rearrange("p (h e) -> p h e", e=MD),
                                        mix_sum[:, :].rearrange("p (h e) -> p h e", e=MD),
                                        h_rden[:, :].unsqueeze(2).to_broadcast([P, MH, MD]), ALU.mult).then_inc(s_mix, 1)

                def head_scores():
                    if H:
                        dve.wait_ge(s_pair, n(h))
                        need(dve, s_shifted, n(h - 1))
                        V.tensor_reduce(score[:, 0:SHIFTS, 0:MH], pair[:, :, :].rearrange("p r (h e) -> p r h e", e=MD),
                                        AX.X, ALU.add).then_inc(s_score, 1)
                    if H:
                        dve.wait_ge(s_score, n(h))
                        V.tensor_copy(score[:, 1:MH // 2, MH:2 * MH], score[:, 1:MH // 2, 0:MH]).then_inc(s_twice, 1)
                    if H:
                        dve.wait_ge(s_twice, n(h))
                        top = MH // 2 - 1
                        V.tensor_copy(score[:, SHIFTS:MH, 0:MH],
                                      bass.AP(score, top * (2 * MH - 1) + MH,
                                              [[2 * MH * MH, P], [-(2 * MH - 1), top], [1, MH]])).then_inc(s_mirror, 1)
                    if H:
                        dve.wait_ge(s_mirror, n(h))
                        V.tensor_reduce(h_max[:, :], score[:, :, 0:MH].rearrange("p r h -> p h r"), AX.X,
                                        ALU.max).then_inc(s_hmax, 1)
                    if H:
                        dve.wait_ge(s_hmax, n(h))
                        need(dve, s_weight, n(h - 1))
                        V.tensor_tensor(shifted[:, :, :], score[:, :, 0:MH],
                                        h_max[:, :].unsqueeze(1).to_broadcast([P, MH, MH]),
                                        ALU.subtract).then_inc(s_shifted, 1)

                if late(s):
                    head_scores()
                    mixed()
                    if s == BATCH + 2:
                        second_choice(EARLY, 1)
                else:
                    mixed()
                    head_scores()
                if s_is(s, BATCH + 1):
                    dve.wait_ge(s_log, 1)
                    dve.wait_ge(s_const, 3)
                    first_choice(EARLY)
                if A:
                    dve.wait_ge(s_k, 2 * n(a))
                    need(dve, s_s_mm, 4 * n(a - 2))
                    V.tensor_copy(k16[0:KEY, ja, :, :], k_one[0:KEY, ja, :, :]).then_inc(s_k16, 1)
                if B:
                    invert(s, 0)
                if B:
                    normalise(s, 0)
                if B:
                    invert(s, 1)
                if A:
                    group_max(a, 0)
                if B:
                    normalise(s, 1)
                if A:
                    group_max(a, 1)
                if B:
                    invert(s, 2)
                if B:
                    normalise(s, 2)
                if A:
                    group_max(a, 2)
                if B:
                    invert(s, 3)
                if B:
                    normalise(s, 3)
                if has(a + 1):
                    dve.wait_ge(s_y_raw, n(a + 1))
                    need(dve, s_kv_mm, n(a))
                    need(dve, s_xy, n(a))
                    V.tensor_scalar(yT[:, :], y_raw[:, :], CLAMP, -CLAMP, ALU.min, ALU.max).then_inc(s_yT, 1)

            slots(dve, slot)

            dve.wait_ge(s_log, 2)
            first_choice(RECENT)
            second_choice(RECENT, 2)
            ROUTE_STEPS["count"] = step(V.tensor_reduce(count[:, :], chosen[:, :, :].rearrange("p t e -> p e t"),
                                                        AX.X, ALU.add))
            step(V.tensor_reduce(r_key[:, :], gates[:, :, :], AX.X, ALU.add))
            step(V.reciprocal(r_max[:, :], r_key[:, :]))
            step(V.tensor_tensor(gates[:, :, :], gates[:, :, :], over_e(r_max[:, :]), ALU.mult))
            step(V.tensor_tensor(gates[:, :, :], gates[:, :, :], chosen[:, :, :], ALU.mult))
            dve.wait_ge(s_cnt_mm, 1)
            step(V.tensor_scalar(keep[:, :], misc[0][:, 0, 0:EXPERTS], float(CAP), None, ALU.is_le))
            ROUTE_STEPS["gates"] = step(V.tensor_tensor(gates[:, :, :], gates[:, :, :], over_t(keep), ALU.mult))
            wide = [P, EXPERTS, EXPERTS]
            step(V.scalar_tensor_tensor(out=key[:, :], in0=keep[:, :], scalar=-float(EXPERTS), in1=index8[:, :],
                                        op0=ALU.mult, op1=ALU.add))
            step(V.tensor_tensor(t88[:, :, :], key[:, :].unsqueeze(1).to_broadcast(wide),
                                 key[:, :].unsqueeze(2).to_broadcast(wide), ALU.is_lt))
            step(V.tensor_reduce(place[:, :], t88[:, :, :], AX.X, ALU.add))
            step(V.tensor_tensor(t88[:, :, :], index8[:, :].unsqueeze(2).to_broadcast(wide),
                                 place[:, :].unsqueeze(1).to_broadcast(wide), ALU.is_equal))
            step(V.tensor_tensor(t88[:, :, :], t88[:, :, :], index8[:, :].unsqueeze(1).to_broadcast(wide), ALU.mult))
            step(V.tensor_reduce(order_f[:, :], t88[:, :, :], AX.X, ALU.add))
            ROUTE_STEPS["order"] = step(V.tensor_copy(order[:, :], order_f[:, :]))
            step(V.tensor_reduce(kept[:, :], keep[:, :], AX.X, ALU.add))
            step(V.tensor_scalar(n_run[:, 0:1], kept[:, :], 2.0, None, ALU.max))
            ROUTE_STEPS["n"] = step(V.tensor_scalar(n_run[:, 1:2], kept[:, :], -1.0, 1.0, ALU.add, ALU.max))

            V.memset(r_key[:, :], 0.0).then_inc(s_e, 2 * QUAD)
            runs = dve.value_load(n_run[0:1, 0:1], min_val=2, max_val=EXPERTS - 1)
            dve.wait_ge(s_x1n, QUADS)
            for q in range(QUADS):
                dve.wait_ge(s_b2_mm, q + 1)
                t = acc_all[:, q * QUAD:(q + 1) * QUAD, :]
                V.tensor_tensor(t, t, bank_b[q % len(bank_b)], ALU.add).then_inc(s_b2, 1)
            dve.wait_ge(s_b2, QUADS)
            with dve.Fori(0, runs) as k:
                with dve.Fori(0, QUADS // 2) as two:
                    q = two * 2
                    for i in range(2):
                        dve.wait_ge(s_gate_now, k + 1)
                        dve.wait_ge(s_e_mm, k * QUADS + q + i + 1)
                        for t in range(QUAD):
                            tile = (q + i) * QUAD + t
                            row = acc_all[:, bass.ds(tile, 1), :].rearrange("p a f -> p (a f)")
                            gate = gate_run[:, :, :].rearrange("p k t -> p (k t)")[:, bass.ds(k * BATCH + tile, 1)]
                            V.scalar_tensor_tensor(out=row, in0=bank_e[i][:, t, :], scalar=gate, in1=row,
                                                   op0=ALU.mult, op1=ALU.add).then_inc(s_e, 1)

        @block.sync
        def _(sp):
            for t, src in ((cond_sb[:, :], condT), (affw_sb[:, :, :], aff_wT), (affb_sb[:, :], aff_b),
                           (modb_sb[:, :], mod_b)):
                sp.dma_start(t, src).then_inc(s_ld_mod, 16)
            sp.dma_start(modw_sb[:, :, :], mod_wT).then_inc(s_ld_modw, 16)
            half = TOKENS // 2
            sp.dma_start(x_all[:, 0:QUAD * P], xT[:, 0:QUAD * P]).then_inc(s_ld_x0, 16)
            sp.dma_start(wk_sb[:, :], wk).then_inc(s_ld_qkv, 16)
            sp.dma_start(wv_sb[:, :], wv).then_inc(s_ld_qkv, 16)
            sp.dma_start(wq_sb[:, :], wq).then_inc(s_ld_qkv, 16)
            sp.dma_start(x_all[:, QUAD * P:half], xT[:, QUAD * P:half]).then_inc(s_ld_x, 16)
            sp.dma_start(x_all[:, half:TOKENS], xT[:, half:TOKENS]).then_inc(s_ld_x, 16)
            sp.dma_start(wpost_sb[:, :, :], wpost.rearrange("(c k) n -> k c n", k=P)).then_inc(s_ld_post, 16)
            sp.dma_start(gate_sb[:, :], gate_wT).then_inc(s_ld_post, 16)
            sp.dma_start(w1_sb[:, :, :], w1.rearrange("e h f -> h e f")).then_inc(s_ld_ffn, 16)
            sp.dma_start(w2_sb[:, :, :], w2.rearrange("e h f -> h e f")).then_inc(s_ld_ffn, 16)
            sp.dma_start(b1_sb[:, :], b1T).then_inc(s_ld_ffn, 16)
            sp.wait_ge(s_zero, 2)
            for i in range(P // EXPERTS):
                sp.dma_start(b2_rows[i * EXPERTS:(i + 1) * EXPERTS, i, :], b2).then_inc(s_ld_ffn, 16)
            sp.wait_ge(s_rt, ROUTE_STEPS["n"])
            before_last = sp.value_load(n_run[0:1, 1:2], min_val=1, max_val=EXPERTS - 1)
            for q in range(QUADS):
                sp.wait_ge(s_e, before_last * (QUADS * QUAD) + (q + 3) * QUAD)
                sp.dma_start(out[q * QUAD * P:(q + 1) * QUAD * P, :].rearrange("(t p) c -> p t c", p=P),
                             acc_all[:, q * QUAD:(q + 1) * QUAD, :]).then_inc(s_out, 16)
            sp.wait_ge(s_out, 16 * QUADS)

        @block.tensor
        def _(pe):
            mm = nc.tensor.matmul

            pe.wait_ge(s_ld_mod, 64)
            for m in range(3):
                last = mm(misc[0][:, 0, m * BATCH:(m + 1) * BATCH], affw_sb[:, m, :], cond_sb[:, :],
                          start=(m == 0), stop=True, skip_group_check=True)
            last.then_inc(s_style_mm, 1)
            pe.wait_ge(s_sq, 2)
            for m in range(3):
                last = mm(misc[1][:, 0, m * BATCH:(m + 1) * BATCH], modw_sq[:, m, :], style_sq[:, m, :],
                          start=(m == 0), stop=True, skip_group_check=True)
            last.then_inc(s_power_mm, 1)
            pe.wait_ge(s_power, 1)
            pe.wait_ge(s_const, 1)
            pe.wait_ge(s_ld_qkv, 48)

            def scores(s, j, g):
                need(pe, s_max, 4 * s + g)
                pe.wait_ge(s_q16, 2 * s + g // 2 + 1)
                for w in range(HPG):
                    last = mm(bank_s[:, w, :], q16[:, j, HPG * g + w, :], k16[:, j, g, :],
                              start=(w == 0), stop=True, skip_group_check=True)
                last.then_inc(s_s_mm, 1)

            def scores_t(s, j, g):
                need(pe, s_prob, 4 * s + g - 1)
                pe.wait_ge(s_own, 4 * s + g + 1)
                mm(bank_t[g % 2][:, :, :], k_one[:, j, g, :], qT[:, j, HPG * g:HPG * (g + 1), :],
                   start=True, stop=True).then_inc(s_t_mm, 1)

            def attend(s, j, g):
                pe.wait_ge(s_prob, 4 * s + g + 1)
                need(pe, s_att, 4 * s + g - 1)
                for w in range(HPG):
                    last = mm(att_bank(g)[:, w, :], prob[:, g % 2, w, :], v1[:, j, g, :],
                              start=(w == 0), stop=True, skip_group_check=True)
                last.then_inc(s_av_mm, 1)

            def queries(b, half):
                bank = qkv_bank(b, ("q0", "q1")[half])
                for c in range(4 * half, 4 * half + 4):
                    last = mm(bank[:, c % 4, :], wq_sb[:, c * P:(c + 1) * P], yT[:, :],
                              start=(c % 4 == 0), stop=True, skip_group_check=True)
                last.then_inc(s_q_mm, 1)

            def att_transpose(b, half):
                pe.wait_ge(s_att, 4 * b + 2 * half + 2)
                for c in range(4 * half, 4 * half + 4):
                    last = nc.tensor.transpose(misc[1 + half][:, c % 4, :],
                                               att[:, 2 * c:2 * c + 2, :].rearrange("p h e -> p (h e)"),
                                               ident[:, :])
                last.then_inc(s_attT_mm, 1)

            early_ends = (0, 6, 10, 15, 20, 24, len(EARLY))
            parts_early = [EARLY[a:b] for a, b in zip(early_ends, early_ends[1:])]

            def gate_logits(tiles):
                bank = bank_s if tiles[0] in EARLY else misc[0]
                pe.wait_ge(s_tok, tiles[-1] + 1)
                for b in tiles:
                    last = mm(bank[:, :, :].rearrange("p w f -> p (w f)")[:, b * EXPERTS:(b + 1) * EXPERTS],
                              tok_all[:, col(b)], gate_sb[:, :], start=(b in (EARLY[0], RECENT[0])), stop=True,
                              skip_group_check=True)
                last.then_inc(s_log_mm, 1)

            def x1_transpose(quads):
                pe.wait_ge(s_x1T, BATCH)
                for q in quads:
                    need(pe, s_x1n, q - 3)
                    for t in range(QUAD):
                        last = nc.tensor.transpose(bank_x[q % 4][:, t, :], x_all[:, col(q * QUAD + t)], ident[:, :])
                    last.then_inc(s_x1n_mm, 1)

            def slot(s, j):
                a, c, h, d = s + 1, s - 1, s - 2, s - 3
                A, B, C, H, D = has(a), has(s), has(c), has(h), has(d)
                ja = 1 - j
                if s_is(s, BATCH + 2):
                    gate_logits(RECENT[:-1])
                if C:
                    bank_free(pe, 1, s, "att0")
                    att_transpose(c, 0)
                if B:
                    scores(s, j, 3)
                if C:
                    bank_free(pe, 2, s, "att1")
                    att_transpose(c, 1)
                if s_is(s, BATCH):
                    gate_logits(parts_early[2])
                if A:
                    pe.wait_ge(s_yT, n(a))
                    queries(a, 0)
                if B:
                    bank_free(pe, 1, s, "neg")
                    pe.wait_ge(s_max, 4 * s + 4)
                    nc.tensor.transpose(misc[1][:, 0, :], row_max[:, :], ident[:, :]).then_inc(s_neg_mm, 1)
                if s_is(s, BATCH - 1):
                    gate_logits(parts_early[0])
                if C:
                    if isinstance(s, int) and c == 0:
                        pe.wait_ge(s_ld_post, 32)
                    pe.wait_ge(s_attT, 2 * n(c))
                    for k in range(CHUNKS):
                        last = mm(misc[2][:, 0, :], wpost_sb[:, k, :], attT[:, k, :],
                                  start=(k == 0), stop=(k == CHUNKS - 1))
                    last.then_inc(s_post_mm, 1)
                if s_is(s, BATCH):
                    gate_logits(parts_early[3])
                if B:
                    scores_t(s, j, 0)
                if A:
                    if not s_is(a, 0):
                        bank_free(pe, 0, s, "q1")
                    queries(a, 1)
                if C:
                    bank_free(pe, 1, s, "kx")
                    pe.wait_ge(s_x1s, n(c))
                    mm(misc[1][:, 0, :], modw_sb[:, 1, :], x1s[:, :], start=True, stop=True).then_inc(s_kx_mm, 1)
                if s_is(s, BATCH):
                    gate_logits(parts_early[4])
                if B:
                    scores_t(s, j, 1)
                if C:
                    pe.wait_ge(s_kxT, n(c))
                    nc.tensor.transpose(misc[1][:, 0, :], kxT[:, :], ident[:, :]).then_inc(s_kxn_mm, 1)
                if D:
                    bank_free(pe, 2, s, "mix")
                    pe.wait_ge(s_mix, n(d))
                    nc.tensor.transpose(misc[2][:, 0, :], mix[:, :], ident[:, :]).then_inc(s_mixT_mm, 1)
                if s_is(s, BATCH):
                    gate_logits(parts_early[5])
                if B:
                    attend(s, j, 0)
                if s_is(s, BATCH - 1):
                    gate_logits(parts_early[1])
                if A:
                    if not s_is(a, 0):
                        bank_free(pe, 0, s, "kv")
                    bank = qkv_bank(a, "kv")
                    for i in range(2):
                        mm(bank[:, i, :], wk_sb[:, i * P:(i + 1) * P], yT[:, :],
                           start=(i == 0), stop=True, skip_group_check=True)
                    mm(bank[:, 2:4, :].rearrange("p a f -> p (a f)"), yT[:, :], wv_sb[:, :], start=False,
                       stop=True, skip_group_check=True).then_inc(s_kv_mm, 1)
                if D:
                    bank_free(pe, 1, s, "o")
                    pe.wait_ge(s_mixT, n(d))
                    mm(misc[1][:, 0, :], modw_sb[:, 2, :], mixT[:, :], start=True, stop=True).then_inc(s_o_mm, 1)
                if B:
                    scores_t(s, j, 2)
                if B:
                    attend(s, j, 1)
                if A:
                    pe.wait_ge(s_k16, n(a))
                    scores(a, ja, 0)
                if B:
                    scores_t(s, j, 3)
                if A:
                    scores(a, ja, 1)
                if B:
                    attend(s, j, 2)
                if A:
                    scores(a, ja, 2)
                if B:
                    attend(s, j, 3)
                if has(a + 1):
                    bank_free(pe, 0, s, "y")
                    pe.wait_ge(s_xs, n(a + 1))
                    mm(misc[0][:, 0, :], modw_sb[:, 0, :], xs[:, j, :], start=True, stop=True).then_inc(s_y_mm, 1)
                if s_is(s, BATCH + 2):
                    gate_logits(RECENT[-1:])
                    x1_transpose(range(QUADS // 2))

            slots(pe, slot)

            pe.wait_ge(s_log, 2)
            pe.wait_ge(s_rt, ROUTE_STEPS["count"])
            mm(misc[0][:, 0, 0:EXPERTS], ones[:, :], count[:, :], start=True, stop=True).then_inc(s_cnt_mm, 1)
            x1_transpose(range(QUADS // 2, QUADS))
            pe.wait_ge(s_rt, ROUTE_STEPS["gates"])
            for i in range(2):
                src = gates[:, i * 16:(i + 1) * 16, :].rearrange("p t e -> p (t e)")
                last = nc.tensor.transpose(misc[1][:, i, :], src, ident[:, :])
            last.then_inc(s_gT_mm, 1)
            pe.wait_ge(s_gT, 1)
            pe.wait_ge(s_x1n, QUADS)
            pe.wait_ge(s_ld_ffn, 16 * (3 + P // EXPERTS))
            for q in range(QUADS):
                need(pe, s_b2, q - len(bank_b) + 1)
                i = q * QUAD
                mm(bank_b[q % len(bank_b)], gatesT[:, i // 16, :],
                   b2_rows[:, i % 16:i % 16 + QUAD, :],
                   start=True, stop=True).then_inc(s_b2_mm, 1)

            def hidden(q, i):
                mm(bank_t[i][:, :, :], w1_now[:, :], tok_all[:, bass.ds(q * QUAD * P, QUAD * P)],
                   start=True, stop=True).then_inc(s_h_mm, 1)

            def output(k, q, i):
                pe.wait_ge(s_w2_now, k + 1)
                pe.wait_ge(s_h, k * QUADS + q + 1)
                pe.wait_ge(s_e, (k * QUADS + q + 1) * QUAD)
                for t in range(QUAD):
                    last = mm(bank_e[i][:, t, :], hT[:, i, t * P:(t + 1) * P],
                              w2_run[:, bass.ds(k, 1), :].rearrange("p a f -> p (a f)"),
                              start=(t == 0), stop=True, skip_group_check=True)
                last.then_inc(s_e_mm, 1)

            pe.wait_ge(s_tok, BATCH)
            pe.wait_ge(s_rt, ROUTE_STEPS["n"])
            runs = pe.value_load(n_run[0:1, 0:1], min_val=2, max_val=EXPERTS - 1)
            pe.wait_ge(s_w1, 1)
            hidden(0, 0)
            hidden(1, 1)
            with pe.Fori(0, runs) as k:
                with pe.Fori(0, QUADS // 2 - 1) as two:
                    for i in range(2):
                        output(k, two * 2 + i, i)
                        hidden(two * 2 + (2 + i), i)
                for i in range(2):
                    output(k, QUADS - 2 + i, i)
                pe.wait_ge(s_w1, k + 2)
                for i in range(2):
                    hidden(i, i)

        @block.scalar
        def _(act):
            def f(out_, in_, func=ACT.Copy, **kw):
                return nc.scalar.activation(out_, in_, func, **kw)

            act.wait_ge(s_zero, 1)
            f(y_raw[:, 0:1], ones[:, 0:1], ACT.Sqrt).then_inc(s_warm, 1)
            act.wait_ge(s_warm, 1)
            act.wait_ge(s_ld_mod, 64)
            act.wait_ge(s_style_mm, 1)
            gains = (1.0 / COND ** 0.5, 1.0, 1.0)
            for m in range(3):
                f(style[:, m, :], misc[0][:, 0, m * BATCH:(m + 1) * BATCH], ACT.Identity,
                  bias=affb_sb[:, m:m + 1], scale=gains[m]).then_inc(s_style, 1)
            act.wait_ge(s_power, 1)
            f(root[:, :, :], power[:, :, :], ACT.Sqrt).then_inc(s_root, 1)
            act.wait_ge(s_demod, 5)
            act.wait_ge(s_zero, 7)
            act.wait_ge(s_blank, 4)

            def exp_scores(s, g):
                act.wait_ge(s_t_mm, 4 * s + g + 1)
                need(act, s_av_mm, 4 * s + g - 1)
                f(prob[:, g % 2, :, :], bank_t[g % 2][:, :, :], ACT.Exp, scale=KEY_SCALE).then_inc(s_prob, 1)

            def copy_q(b, j, half):
                act.wait_ge(s_q_mm, 2 * b + half + 1)
                need(act, s_t_mm, 4 * n(b - 2))
                need(act, s_q16, n(b - 2))
                for par in range(2):
                    f(qT[0:KEY, j, HEADS // 2 * half + par:HEADS // 2 * (half + 1):2, :],
                      qkv_bank(b, ("q0", "q1")[half])[par * KEY:(par + 1) * KEY, :, :]).then_inc(s_q, 1)

            def copy_att(b, half):
                need(act, s_post_mm, n(b - 1))
                act.wait_ge(s_attT_mm, 2 * b + half + 1)
                f(attT[:, 4 * half:4 * half + 4, :], misc[1 + half][:, :, :]).then_inc(s_attT, 1)

            def route_exp(tiles):
                act.wait_ge(s_rt, ROUTE_STEPS["exp", tiles[0]])
                f(gates[:, tiles[0]:tiles[-1] + 1, :], rest[:, tiles[0]:tiles[-1] + 1, :], ACT.Exp).then_inc(s_rt_exp, 1)

            def copy_logits(tiles, products):
                act.wait_ge(s_log_mm, products)
                bank = bank_s if tiles[0] in EARLY else misc[0]
                cols = slice(tiles[0] * EXPERTS, (tiles[-1] + 1) * EXPERTS)
                f(logits[:, tiles[0]:tiles[-1] + 1, :].rearrange("p t e -> p (t e)"),
                  bank[:, :, :].rearrange("p w f -> p (w f)")[:, cols]).then_inc(s_log, 1)

            def copy_x1(quads):
                for q in quads:
                    act.wait_ge(s_x1n_mm, q + 1)
                    f(acc_all[:, q * QUAD:(q + 1) * QUAD, :], bank_x[q % 4]).then_inc(s_x1n, 1)

            def narrow_q(b, j, half):
                act.wait_ge(s_q, 4 * b + 2 * half + 2)
                need(act, s_s_mm, 4 * n(b - 2))
                heads = slice(HEADS // 2 * half, HEADS // 2 * (half + 1))
                f(q16[0:KEY, j, heads, :], qT[0:KEY, j, heads, :]).then_inc(s_q16, 1)

            def slot(s, j):
                a, c, h, d = s + 1, s - 1, s - 2, s - 3
                A, B, C, H, D = has(a), has(s), has(c), has(h), has(d)
                ja, jc, jh, jd = 1 - j, 1 - j, j, 1 - j
                def head_weights():
                    if H:
                        act.wait_ge(s_shifted, n(h))
                        need(act, s_mix, n(h - 2))
                        need(act, s_hi, 4 * n(h - 2))
                        f(weight[:, jh, :, :], shifted[:, :, :], ACT.Exp, scale=MIX_SCALE).then_inc(s_weight, 1)

                if late(s):
                    head_weights()
                if s_is(s, BATCH + 1):
                    route_exp(EARLY)
                if C:
                    copy_att(c, 0)
                    copy_att(c, 1)
                if B:
                    act.wait_ge(s_neg_mm, n(s))
                    need(act, s_own, 4 * n(s - 1))
                    f(neg_max[KEY:KEY + HEADS, :], misc[1][KEY:KEY + HEADS, 0, :], scale=-1.0).then_inc(s_neg, 1)
                if A:
                    copy_q(a, ja, 0)
                    narrow_q(a, ja, 0)
                if C:
                    act.wait_ge(s_x1T, n(c))
                    need(act, s_kx_mm, n(c - 1))
                    act.wait_ge(s_demod, 5)
                    f(x1s[:, :], x_all[:, col(c)], scale=style[:, 1, bass.ds(c, 1)]).then_inc(s_x1s, 1)
                if B:
                    exp_scores(s, 0)
                if C:
                    act.wait_ge(s_kx_mm, n(c))
                    need(act, s_kxn_mm, n(c - 1))
                    act.wait_ge(s_demod, 5)
                    f(kxT[:, :], misc[1][:, 0, :], ACT.Identity, scale=demod[:, 1, bass.ds(c, 1)],
                      bias=modb_sb[:, 1:2]).then_inc(s_kxT, 1)
                if A:
                    copy_q(a, ja, 1)
                if B:
                    exp_scores(s, 1)
                if C:
                    act.wait_ge(s_kxn_mm, n(c))
                    need(act, s_lo, 4 * n(c - 2))
                    need(act, s_hi, 4 * n(c - 2))
                    f(kx2[:, jc, :].rearrange("p (r f) -> p r f", r=2),
                      misc[1][:, 0:1, :].to_broadcast([P, 2, P])).then_inc(s_kx2, 1)
                if D:
                    act.wait_ge(s_mixT_mm, n(d))
                    need(act, s_o_mm, n(d - 1))
                    act.wait_ge(s_style, 3)
                    f(mixT[:, :], misc[2][:, 0, :], scale=style[:, 2, bass.ds(d, 1)]).then_inc(s_mixT, 1)
                if A:
                    act.wait_ge(s_kv_mm, n(a))
                    need(act, s_t_mm, 4 * n(a - 2))
                    need(act, s_k16, n(a - 2))
                    for src in range(2):
                        f(k_one[0:KEY, ja, src:GROUPS:2, :],
                          qkv_bank(a, "kv")[src * KEY:(src + 1) * KEY, 0:2, :]).then_inc(s_k, 1)
                if A:
                    narrow_q(a, ja, 1)
                if s_is(s, BATCH):
                    copy_logits(EARLY, 6)
                if not late(s):
                    head_weights()
                if A:
                    need(act, s_av_mm, 4 * n(a - 2))
                    f(v1[:, ja, :, 0:KEY],
                      qkv_bank(a, "kv")[:, 2:4, :].rearrange("p a (g e) -> p (a g) e", e=KEY)).then_inc(s_v, 1)
                if B:
                    exp_scores(s, 2)
                if D:
                    act.wait_ge(s_o_mm, n(d))
                    act.wait_ge(s_demod, 5)
                    f(tok_all[:, col(d)], misc[1][:, 0, :], ACT.Identity, scale=demod[:, 2, bass.ds(d, 1)],
                      bias=modb_sb[:, 2:3]).then_inc(s_tok, 1)
                if B:
                    exp_scores(s, 3)
                if has(a + 1):
                    act.wait_ge(s_y_mm, n(a + 1))
                    need(act, s_yT, n(a))
                    act.wait_ge(s_demod, 5)
                    f(y_raw[:, :], misc[0][:, 0, :], ACT.Identity, scale=demod[:, 0, bass.ds(a + 1, 1)],
                      bias=modb_sb[:, 0:1]).then_inc(s_y_raw, 1)
                if s_is(s, BATCH + 2):
                    copy_logits(RECENT, 8)

            slots(act, slot)

            route_exp(RECENT)
            copy_x1(range(QUADS))
            act.wait_ge(s_gT_mm, 1)
            f(gatesT[:, :, :], misc[1][:, 0:2, :]).then_inc(s_gT, 1)
            def set_expert(k, e):
                f(gate_run[:, bass.ds(k, 1), :].rearrange("p a t -> p (a t)"),
                  gates[:, :, bass.ds(e, 1)].rearrange("p t a -> p (t a)")).then_inc(s_gate_now, 1)
                f(w2_run[:, bass.ds(k, 1), :], w2_sb[:, bass.ds(e, 1), :]).then_inc(s_w2_now, 1)

            def set_hidden(e):
                f(b1_now[:, :], b1_sb[:, bass.ds(e, 1)]).then_inc(s_b1, 1)
                f(w1_now[:, :], w1_sb[:, bass.ds(e, 1), :].rearrange("p a f -> p (a f)")).then_inc(s_w1, 1)

            def relu(count, i):
                act.wait_ge(s_h_mm, count)
                f(hT[:, i, :], bank_t[i][:, :, :].rearrange("p t f -> p (t f)"), ACT.Relu,
                  bias=b1_now[:, :]).then_inc(s_h, 1)

            act.wait_ge(s_ld_ffn, 16 * (3 + P // EXPERTS))
            act.wait_ge(s_rt, ROUTE_STEPS["n"])
            e = act.value_load(order[0:1, 0:1], min_val=0, max_val=EXPERTS - 1)
            set_hidden(e)
            set_expert(0, e)
            runs = act.value_load(n_run[0:1, 0:1], min_val=2, max_val=EXPERTS - 1)
            act.wait_ge(s_b1, 1)
            for i in range(2):
                relu(i + 1, i)
            with act.Fori(0, runs) as k:
                e = act.value_load(order[0:1, bass.ds(k + 1, 1)], min_val=0, max_val=EXPERTS - 1)
                set_expert(k + 1, e)
                with act.Fori(0, QUADS // 2 - 1) as two:
                    for i in range(2):
                        relu(k * QUADS + two * 2 + (3 + i), i)
                act.wait_ge(s_h, k * QUADS + QUADS)
                act.wait_ge(s_demod, 5)
                set_hidden(e)
                act.wait_ge(s_b1, k + 2)
                for i in range(2):
                    relu(k * QUADS + (QUADS + 1 + i), i)

        @block.gpsimd
        def _(pool):
            G = nc.gpsimd
            G.memset(ident[:, :], 0.0).then_inc(s_blank, 1)
            G.memset(own_head[:, :], 0.0).then_inc(s_blank, 1)
            pool.wait_ge(s_blank, 2)
            G.affine_select(out=ident[:, :], in_=ident[:, :], compare_op=ALU.not_equal, fill=1.0, base=0,
                            pattern=[[-1, P]], channel_multiplier=1).then_inc(s_const, 1)
            G.affine_select(out=own_head[:, :], in_=own_head[:, :], compare_op=ALU.not_equal, fill=1.0, base=-KEY,
                            pattern=[[-1, HEADS]], channel_multiplier=1).then_inc(s_const, 1)
            pool.wait_ge(s_const, 2)
            G.memset(q16[KEY:P, :, :, :], 0.0).then_inc(s_blank, 1)
            G.memset(qT[KEY:P, :, :, :], 0.0).then_inc(s_blank, 1)
            pool.wait_ge(s_blank, 4)

            pool.wait_ge(s_style, 3)

            def slot(s, j):
                a, c, h, d = s + 1, s - 1, s - 2, s - 3
                A, B, C, H, D = has(a), has(s), has(c), has(h), has(d)
                ja, jc, jh, jd = 1 - j, 1 - j, j, 1 - j

                def xs_of(b, jb):
                    need(pool, s_y_mm, n(b - 2))
                    pool.wait_ge(s_style, 3)
                    G.tensor_tensor(xs[:, jb, :], x_all[:, col(b)],
                                    style[:, 0, bass.ds(b, 1)].to_broadcast([P, P]), ALU.mult).then_inc(s_xs, 1)

                if D:
                    pool.wait_ge(s_weight, n(d))
                    need(pool, s_msum, n(d - 1))
                    G.tensor_tensor(mix_hi[:, :, :].rearrange("p r (h e) -> p r h e", e=MD),
                                    weight[:, jd, MH // 2:MH, :].unsqueeze(3).to_broadcast([P, MH // 2, MH, MD]),
                                    bass.AP(kx2, jd * 2 * P + MD * MH // 2,
                                            [[4 * P, P], [MD, MH // 2], [MD, MH], [1, MD]]),
                                    ALU.mult).then_inc(s_hi, 1)
                    for i, r in enumerate((4, 2, 1)):
                        pool.wait_ge(s_hi, 4 * d + i + 1)
                        G.tensor_tensor(mix_hi[:, 0:r, :], mix_hi[:, 0:r, :], mix_hi[:, r:2 * r, :],
                                        ALU.add).then_inc(s_hi, 1)
                if B:
                    pool.wait_ge(s_neg, n(s))
                    pool.wait_ge(s_const, 2)
                    rows = slice(KEY, KEY + HEADS)
                    if D:
                        pool.wait_ge(s_hi, 4 * n(d))
                    else:
                        pool.wait_ge(s_xs, n(s + 1))
                    for g in range(GROUPS):
                        need(pool, s_own, 4 * s + g)
                        need(pool, s_t_mm, 4 * n(s - 2))
                        heads = slice(HPG * g, HPG * (g + 1))
                        G.tensor_tensor(qT[rows, j, heads, :],
                                        neg_max[rows, :].unsqueeze(1).to_broadcast([HEADS, HPG, P]),
                                        own_head[rows, heads].unsqueeze(2).to_broadcast([HEADS, HPG, P]),
                                        ALU.mult).then_inc(s_own, 1)
                    pool.wait_ge(s_own, 4 * s + 4)
                if C:
                    pool.wait_ge(s_kx2, n(c))
                    need(pool, s_score, n(c - 1))
                    G.tensor_tensor(pair[:, :, :],
                                    bass.AP(kx2, jc * 2 * P, [[4 * P, P], [0, SHIFTS], [1, P]]),
                                    bass.AP(kx2, jc * 2 * P, [[4 * P, P], [MD, SHIFTS], [1, P]]),
                                    ALU.mult).then_inc(s_pair, 1)
                if isinstance(s, int) and s == -2:
                    pool.wait_ge(s_ld_x0, 16)
                if isinstance(s, int) and s + 2 == QUAD:
                    pool.wait_ge(s_ld_x, 32)
                if has(s + 2):
                    xs_of(s + 2, j)
                if isinstance(s, int) and s == 0:
                    for e in range(EXPERTS):
                        G.memset(index8[:, e:e + 1], float(e))
                        last = G.memset(rank8[:, e:e + 1], float(EXPERTS - e))
                    last.then_inc(s_const, 1)
                    pool.wait_ge(s_const, 3)

            slots(pool, slot)


_INS = ("xT", "condT", "aff_wT", "aff_b", "mod_wT", "mod_b", "wq", "wk", "wv", "wpost", "gate_wT",
        "w1", "b1T", "w2", "b2")


def kernel(x, cond_512, L0_cond_weight, L0_cond_bias, L0_cond_affine_w, L0_cond_affine_b, L0_attn_Wq,
           L0_attn_Wk, L0_attn_Wv, L0_attn_Wpost, L0_cond2_k_aff_w, L0_cond2_k_aff_b, L0_cond2_k_w,
           L0_cond2_k_b, L0_cond2_o_aff_w, L0_cond2_o_aff_b, L0_cond2_o_w, L0_cond2_o_b, L0_ffn_gate_w,
           L0_ffn_W1, L0_ffn_b1, L0_ffn_W2, L0_ffn_b2):
    import concourse.bacc as bacc
    from concourse.bass_utils import run_bass_kernel_spmd

    arrays = {
        "xT": np.asarray(x).reshape(TOKENS, P).T,
        "condT": np.asarray(cond_512).T,
        "aff_wT": np.stack([np.asarray(w).T for w in (L0_cond_affine_w, L0_cond2_k_aff_w, L0_cond2_o_aff_w)], 1),
        "aff_b": np.stack([np.asarray(w) for w in (L0_cond_affine_b, L0_cond2_k_aff_b, L0_cond2_o_aff_b)], 1),
        "mod_wT": np.stack([np.asarray(w).T for w in (L0_cond_weight, L0_cond2_k_w, L0_cond2_o_w)], 1),
        "mod_b": np.stack([np.asarray(w) for w in (L0_cond_bias, L0_cond2_k_b, L0_cond2_o_b)], 1),
        "wq": L0_attn_Wq, "wk": L0_attn_Wk, "wv": L0_attn_Wv, "wpost": L0_attn_Wpost,
        "gate_wT": np.asarray(L0_ffn_gate_w).T,
        "w1": L0_ffn_W1, "b1T": np.asarray(L0_ffn_b1).T, "w2": L0_ffn_W2, "b2": L0_ffn_b2,
    }
    arrays = {k: np.ascontiguousarray(v) for k, v in arrays.items()}
    nc = bacc.Bacc("TRN2", target_bir_lowering=False, num_devices=1)
    ins = [nc.dram_tensor(f"in_{k}", arrays[k].shape, mybir.dt.from_np(arrays[k].dtype),
                          kind="ExternalInput").ap() for k in _INS]
    out = nc.dram_tensor("out", (TOKENS, P), F32, kind="ExternalOutput").ap()
    build(nc, *ins, out)
    result = run_bass_kernel_spmd(nc, [{f"in_{k}": arrays[k] for k in _INS}], core_ids=[0])
    return result.results[0]["out"].reshape(BATCH, P, P)
```
